# Optimizing a Trainium2 kernel written in Bass

```python
import numpy as np
import jax
import jax.numpy as jnp

def _softmax(x, axis=-1):
    return jax.nn.softmax(x, axis=axis)

def _gelu(x):
    return jax.nn.gelu(x, approximate=True)

def _silu(x):
    return jax.nn.silu(x)

def _sigmoid(x):
    return jax.nn.sigmoid(x)

def _layernorm(x, axis=-1, eps=1e-05):
    m = jnp.mean(x, axis=axis, keepdims=True)
    v = jnp.var(x, axis=axis, keepdims=True)
    return (x - m) / jnp.sqrt(v + eps)

def _scatter_add(tgt, idx, src, axis=0):
    return tgt.at[idx].add(src)

def _segment_sum(src, seg, n):
    return jax.ops.segment_sum(src, seg, n)
kernel_name = 'mk_sandwich_d1_jaxref_r4_8ac30d'

def setup_inputs(seed: int=0):
    np.random.seed(seed)
    _w = jnp.asarray

    def _L0_attn_setup():
        import jax, jax.numpy as jnp
        import numpy as np
        B, S, E, H, L = (2, 512, 512, 16, 128)
        HD = E // H

        def _reference_tuple_inner(x, Wq, Wdkv, Wuk, Wuv, ln_g, ln_b, Wo_h, Wo, bo):
            Bx, Sx, Ex = x.shape
            xh = x.reshape(Bx, Sx, H, HD).transpose(0, 2, 1, 3)
            c = jnp.einsum('bhsd,hld->bhsl', xh, Wdkv)
            mu = c.mean(-1, keepdims=True)
            var = c.var(-1, keepdims=True)
            c = (c - mu) * jax.lax.rsqrt(var + 1e-05)
            c = c * ln_g[None, :, None, :] + ln_b[None, :, None, :]
            absorbed = jnp.einsum('hij,hlj->hil', Wq, Wuk)
            q_lat = jnp.einsum('bhsd,hdl->bhsl', xh, absorbed)
            scores = jnp.einsum('bhsl,bhtl->bhst', q_lat, c)
            scores = scores * (1.0 / np.sqrt(L).astype(np.float32))
            mask = jnp.tril(jnp.ones((Sx, Sx), dtype=bool))
            scores = jnp.where(mask, scores, -jnp.inf)
            w = jax.nn.softmax(scores, axis=-1)
            v = jnp.einsum('bhsl,hld->bhsd', c, Wuv)
            oh = jnp.einsum('bhst,bhtd->bhsd', w, v)
            oh = jnp.einsum('bhsd,hed->bhse', oh, Wo_h)
            o = oh.transpose(0, 2, 1, 3).reshape(Bx, Sx, Ex)
            out = o @ Wo.T + bo
            return (out, c)
        key = jax.random.key(seed)
        ks = jax.random.split(key, 8)
        sd = 0.02
        return {'x': jax.random.normal(ks[0], (B, S, E), jnp.float32), 'Wq': jax.random.normal(ks[1], (H, HD, HD), jnp.float32) * sd, 'Wdkv': jax.random.normal(ks[2], (H, L, HD), jnp.float32) * sd, 'Wuk': jax.random.normal(ks[3], (H, L, HD), jnp.float32) * sd, 'Wuv': jax.random.normal(ks[4], (H, L, HD), jnp.float32) * sd, 'ln_g': jnp.ones((H, L), jnp.float32), 'ln_b': jnp.zeros((H, L), jnp.float32), 'Wo_h': jax.random.normal(ks[5], (H, HD, HD), jnp.float32) * sd, 'Wo': jax.random.normal(ks[6], (E, E), jnp.float32) * sd, 'bo': jnp.zeros((E,), jnp.float32)}
    _L0_attn_in = _L0_attn_setup()

    def _L0_ffn_setup():
        import jax, jax.numpy as jnp
        import numpy as np
        HIDDEN = 512
        INTER = 2048
        B, S = (4, 256)

        def _qmatmul(x, w_int8, scale):
            y = jnp.einsum('bsh,ho->bso', x, w_int8.astype(x.dtype))
            return y * scale
        key = jax.random.key(seed)
        ks = jax.random.split(key, 7)
        x = jax.random.normal(ks[0], (B, S, HIDDEN), dtype=jnp.float32)
        w_gate = jax.random.randint(ks[1], (HIDDEN, INTER), -128, 128, dtype=jnp.int32).astype(jnp.int8)
        w_up = jax.random.randint(ks[2], (HIDDEN, INTER), -128, 128, dtype=jnp.int32).astype(jnp.int8)
        w_down = jax.random.randint(ks[3], (INTER, HIDDEN), -128, 128, dtype=jnp.int32).astype(jnp.int8)
        s_gate = jax.random.uniform(ks[4], (INTER,), dtype=jnp.float32) * 0.02 + 0.001
        s_up = jax.random.uniform(ks[5], (INTER,), dtype=jnp.float32) * 0.02 + 0.001
        s_down = jax.random.uniform(ks[6], (HIDDEN,), dtype=jnp.float32) * 0.02 + 0.001
        return {'x': x, 'w_gate': w_gate, 'w_up': w_up, 'w_down': w_down, 's_gate': s_gate, 's_up': s_up, 's_down': s_down}
    _L0_ffn_in = _L0_ffn_setup()
    _d = {'L0_attn_x': _L0_attn_in['x'], 'L0_attn_Wq': _L0_attn_in['Wq'], 'L0_attn_Wdkv': _L0_attn_in['Wdkv'], 'L0_attn_Wuk': _L0_attn_in['Wuk'], 'L0_attn_Wuv': _L0_attn_in['Wuv'], 'L0_attn_ln_g': _L0_attn_in['ln_g'], 'L0_attn_ln_b': _L0_attn_in['ln_b'], 'L0_attn_Wo_h': _L0_attn_in['Wo_h'], 'L0_attn_Wo': _L0_attn_in['Wo'], 'L0_attn_bo': _L0_attn_in['bo'], 'L0_ffn_w_gate': _L0_ffn_in['w_gate'], 'L0_ffn_w_up': _L0_ffn_in['w_up'], 'L0_ffn_w_down': _L0_ffn_in['w_down'], 'L0_ffn_s_gate': _L0_ffn_in['s_gate'], 'L0_ffn_s_up': _L0_ffn_in['s_up'], 'L0_ffn_s_down': _L0_ffn_in['s_down']}
    _x0 = _d['L0_attn_x']
    _d['L0_attn_x'] = jax.random.normal(jax.random.fold_in(jax.random.key(seed), 1), (4, 512, 512), dtype=_x0.dtype)
    del _x0
    return _d

def reference(L0_attn_x, L0_attn_Wq, L0_attn_Wdkv, L0_attn_Wuk, L0_attn_Wuv, L0_attn_ln_g, L0_attn_ln_b, L0_attn_Wo_h, L0_attn_Wo, L0_attn_bo, L0_ffn_w_gate, L0_ffn_w_up, L0_ffn_w_down, L0_ffn_s_gate, L0_ffn_s_up, L0_ffn_s_down):

    def _L0_attn_ref(x, Wq, Wdkv, Wuk, Wuv, ln_g, ln_b, Wo_h, Wo, bo):
        import jax, jax.numpy as jnp
        import numpy as np
        B, S, E, H, L = (2, 512, 512, 16, 128)
        HD = E // H

        def _reference_tuple_inner(x, Wq, Wdkv, Wuk, Wuv, ln_g, ln_b, Wo_h, Wo, bo):
            Bx, Sx, Ex = x.shape
            xh = x.reshape(Bx, Sx, H, HD).transpose(0, 2, 1, 3)
            c = jnp.einsum('bhsd,hld->bhsl', xh, Wdkv)
            mu = c.mean(-1, keepdims=True)
            var = c.var(-1, keepdims=True)
            c = (c - mu) * jax.lax.rsqrt(var + 1e-05)
            c = c * ln_g[None, :, None, :] + ln_b[None, :, None, :]
            absorbed = jnp.einsum('hij,hlj->hil', Wq, Wuk)
            q_lat = jnp.einsum('bhsd,hdl->bhsl', xh, absorbed)
            scores = jnp.einsum('bhsl,bhtl->bhst', q_lat, c)
            scores = scores * (1.0 / np.sqrt(L).astype(np.float32))
            mask = jnp.tril(jnp.ones((Sx, Sx), dtype=bool))
            scores = jnp.where(mask, scores, -jnp.inf)
            w = jax.nn.softmax(scores, axis=-1)
            v = jnp.einsum('bhsl,hld->bhsd', c, Wuv)
            oh = jnp.einsum('bhst,bhtd->bhsd', w, v)
            oh = jnp.einsum('bhsd,hed->bhse', oh, Wo_h)
            o = oh.transpose(0, 2, 1, 3).reshape(Bx, Sx, Ex)
            out = o @ Wo.T + bo
            return (out, c)
        return _reference_tuple_inner(x, Wq, Wdkv, Wuk, Wuv, ln_g, ln_b, Wo_h, Wo, bo)[0]

    def _L0_ffn_ref(x, w_gate, w_up, w_down, s_gate, s_up, s_down):
        import jax, jax.numpy as jnp
        import numpy as np
        HIDDEN = 512
        INTER = 2048
        B, S = (4, 256)

        def _qmatmul(x, w_int8, scale):
            y = jnp.einsum('bsh,ho->bso', x, w_int8.astype(x.dtype))
            return y * scale
        gate = jax.nn.silu(_qmatmul(x, w_gate, s_gate))
        up = _qmatmul(x, w_up, s_up)
        fuse = gate * up
        return _qmatmul(fuse, w_down, s_down)
    x = L0_attn_x
    x = x + _layernorm(_L0_attn_ref(_layernorm(x, axis=-1), L0_attn_Wq, L0_attn_Wdkv, L0_attn_Wuk, L0_attn_Wuv, L0_attn_ln_g, L0_attn_ln_b, L0_attn_Wo_h, L0_attn_Wo, L0_attn_bo), axis=-1)
    x = x + _layernorm(_L0_ffn_ref(_layernorm(x, axis=-1), L0_ffn_w_gate, L0_ffn_w_up, L0_ffn_w_down, L0_ffn_s_gate, L0_ffn_s_up, L0_ffn_s_down), axis=-1)
    return x

_drawn_inputs = setup_inputs


def setup_inputs(seed=0):
    import zlib

    import numpy as np

    out = dict(_drawn_inputs(seed))
    spreads = {'L0_attn_ln_g': (1.0, 0.6), 'L0_attn_ln_b': (0.0, 0.759), 'L0_attn_bo': (0.0, 0.1)}
    factors = {'L0_attn_Wq': 8.0,
     'L0_attn_Wdkv': 4.811,
     'L0_attn_Wuk': 8.0,
     'L0_attn_Wuv': 3.682,
     'L0_attn_Wo_h': 3.725,
     'L0_attn_Wo': 3.603}
    for name, (base, spread) in spreads.items():
        noise = np.random.default_rng([zlib.crc32(name.encode()), seed]).standard_normal(out[name].shape)
        drawn = base * np.exp(spread * noise) if base else spread * noise
        out[name] = jnp.asarray(drawn.astype(out[name].dtype))
    for name, factor in factors.items():
        out[name] = (out[name] * factor).astype(out[name].dtype)
    return out
```

```python
import math
from contextlib import ExitStack

import concourse.bass as bass
from concourse import mybir

P = 128
BATCH, SEQ, EMB = 4, 512, 512
HEADS, HD, LAT = 16, 32, 128
INTER = 2048
TOKENS = BATCH * SEQ
TILES = TOKENS // P
SEQ_TILES = SEQ // P
UNITS = BATCH * HEADS
GROUPS = EMB // P
GH = P // HD
ITILES = INTER // P
CHUNK = 512
CTILES = CHUNK // P
STACK = 3 * HD
EPS = 1e-5
VW = HD + 1
X2_SCALE = 2048.0
KEY_BOUND = 256.0
LATENT_MAX = 11.5
FUSE_BOUND = 32000.0
RAW_BOUND = 2.0 ** 16
NEG = -1e30

SETUP_PE = ["mean", "wukT", "wuvT", "vecT", "bdqT", "bdoT", "A", "U", "G", "M", "N", "keybound", "keybias",
            "vb", "woT0", "woT1", "woT2", "woT3", "fuseT", "fuseall", "bo"]
SETUP_DVE = ["ones", "bdzero", "gmnzero", "Wc", "wukT", "vecT", "bdqT", "gA", "bA", "absA", "gU", "bU",
             "G", "M", "N", "keybias", "vb", "fusemax", "fusered", "fusescale", "bo", "done"]
SETUP_ACT = ["wuvT", "bdoT", "woT0", "woT1", "woT2", "woT3"]


def nth(order, name):
    return order.index(name) + 1


class Step:

    def __init__(self, unit, loop, const):
        self.unit, self.loop, self.const = unit, loop, const

    def minus(self, lag):
        return Step(self.unit, self.loop, self.const - lag)

    def times(self, k, plus=0):
        whole = k * self.const + plus
        return whole if self.loop is None else self.loop * (k * self.unit) + whole

    @property
    def parity(self):
        return self.const % 2

    @property
    def batch(self):
        q = self.const // self.unit
        return q if self.loop is None else self.loop + q

    @property
    def sub(self):
        return self.const % self.unit


def wait(eng, sem, value):
    if isinstance(value, int) and value <= 0:
        return
    eng.wait_ge(sem, value)


def wait_apart(eng, sem, value, tally):
    if isinstance(value, int) and value <= 0:
        return
    eng.wait_ge(sem, value)
    eng.sem_inc(tally, 1)


def pipelined(eng, n, unit, stages):
    peel = 4
    deepest = max(lag for lag, _ in stages)

    def step(s, base):
        for lag, fn in stages:
            at = s.minus(lag)
            if base is None or 0 <= base - lag < n:
                fn(at)

    for s in range(peel):
        step(Step(unit, None, s), s)
    with eng.Fori(peel // unit, n // unit) as loop:
        for u in range(unit):
            step(Step(unit, loop, u), None)
    for s in range(n, n + deepest):
        step(Step(unit, None, s), s)


def block_kernel(nc, x, Wq, Wdkv, Wuk, Wuv, ln_g, ln_b, Wo_h, Wo, bo, w_gate, w_up, w_down,
                 s_gate, s_up, s_down, out):
    f32, f16, bf16 = mybir.dt.float32, mybir.dt.float16, mybir.dt.bfloat16
    ALU, ACT, AX = mybir.AluOpType, mybir.ActivationFunctionType, mybir.AxisListType
    ctx = ExitStack()
    with ctx:
        def sb(name, shape, dt):
            return ctx.enter_context(nc.sbuf_tensor(name, shape, dt))

        def sem(name):
            return ctx.enter_context(nc.semaphore(name))

        ident = sb("ident", [P, P], f32)
        ident16 = sb("ident16", [P, P], f16)
        identb = sb("identb", [P, P], bf16)
        causalT = sb("causalT", [P, P], bf16)
        ones = sb("ones", [P, P], f32)
        headsum = sb("headsum", [P, GH], f32)
        halfneg = sb("halfneg", [P, 1], f32)
        vec = sb("vec", [P, 4 * HEADS], f32)
        sgate = sb("sgate", [P, ITILES], f32)
        sup = sb("sup", [P, ITILES], f32)
        kscale = sb("kscale", [P, 4], f32)
        small = sb("small", [P, 2, 96], f32)
        negmax = sb("negmax", [P, 2, SEQ_TILES, HD], f16)
        rowmax = sb("rowmax", [P, 2, SEQ_TILES], f32)
        rsum = sb("rsum", [P, SEQ_TILES], f32)
        scratch = sb("scratch", [P, 64], f32)
        GMN = sb("GMN", [P, GROUPS, 3, P], f32)
        keybias = sb("keybias", [P, EMB], f32)
        WoT = sb("WoT", [P, GROUPS, EMB], f32)
        bo_all = sb("bo_all", [P, EMB], f32)
        sdown = sb("sdown", [P, EMB], f32)
        TMP = sb("TMP", [P, 4736], f32)
        Q = sb("Q", [P, UNITS * SEQ_TILES * STACK], f16)
        K = sb("K", [P, UNITS * SEQ_TILES * STACK], f16)
        V = sb("V", [P, UNITS * SEQ_TILES * VW], f32)
        O = sb("O", [P, UNITS * SEQ_TILES * HD], f32)
        qst = Q[:, :].rearrange("p (n s c) -> p n s c", s=SEQ_TILES, c=STACK)
        kst = K[:, :].rearrange("p (n s c) -> p n s c", s=SEQ_TILES, c=STACK)
        vst = V[:, :].rearrange("p (n s c) -> p n s c", s=SEQ_TILES, c=VW)
        ost = O[:, :].rearrange("p (n s c) -> p n s c", s=SEQ_TILES, c=HD)

        def carve(t, start, shape, dt=f32):
            n = math.prod(shape)
            words = n if dt == f32 else n // 2
            v = t[:, start:start + words]
            v = v if dt == f32 else v.bitcast(dt)
            names = "abcd"[:len(shape)]
            return v.rearrange(f"p ({' '.join(names)}) -> p {' '.join(names)}",
                               **{k: s for k, s in zip(names[1:], shape[1:])}) if len(shape) > 1 else v

        wdkv_sb = carve(O, 0, [EMB])
        wuk_sb = carve(O, 512, [EMB])
        wuv_sb = carve(O, 1024, [EMB])
        bdq = carve(O, 1536, [GROUPS, P])
        bdo = carve(O, 2048, [GROUPS, P])
        wo_nat = carve(O, 2560, [GROUPS, EMB])
        bdqT = carve(O, 4608, [GROUPS, P])
        bdoT = carve(O, 5120, [GROUPS, P])
        wukT = carve(O, 5632, [GROUPS, P])
        wuvT = carve(O, 6144, [GROUPS, P])
        wc = carve(O, 6656, [EMB])
        vb_sb = carve(O, 7168, [GROUPS, P])
        vec_rows = carve(O, 7680, [P])
        gA, bA, absA, gU, bU = (carve(V, 512 * n, [EMB]) for n in range(5))
        p_x = carve(TMP, 0, [2, EMB])
        p_ln = carve(TMP, 1024, [2, EMB])
        p_xT = carve(TMP, 2048, [2, GROUPS, P])
        p_prod = carve(TMP, 3072, [GROUPS, P])
        p_key = carve(TMP, 3584, [2, EMB])
        prob = carve(TMP, 0, [2, 1280])
        qk = carve(TMP, 2560, [2, 2, SEQ], f16)
        masked = carve(TMP, 4096, [1280], bf16)
        causal = carve(TMP, 3584, [SEQ])
        o_x = carve(TMP, 0, [2, EMB])
        o_in = carve(TMP, 1024, [2, EMB])
        o_T = carve(TMP, 2048, [2, GROUPS, P])
        o_y = carve(TMP, 3072, [2, EMB])
        gmn_flat = GMN[:, :, :, :].rearrange("p g m c -> p (g m c)")
        o_x2 = gmn_flat[:, 0:EMB]
        o_parts = gmn_flat[:, EMB:3 * EMB].bitcast(f16).rearrange("p (b h c) -> p b h c", b=2, h=2)
        w_gu = V[:, 0:2 * GROUPS * INTER // 2].bitcast(f16).rearrange("p (m k n) -> p m k n", m=2, k=GROUPS)
        x2T = K[:, 0:2 * GROUPS * TOKENS].rearrange("p (h k t) -> p (h k) t", h=2, k=GROUPS)
        fused = Q[:, 0:2 * ITILES * CHUNK].rearrange("p (h i t) -> p h i t", h=2, i=ITILES)
        w_dn = Q[:, 2 * ITILES * CHUNK:3 * ITILES * CHUNK].rearrange("p (i n) -> p i n", i=ITILES)
        f_silu = carve(TMP, 0, [2, CHUNK])
        f_prod = carve(TMP, 1024, [2, CHUNK])
        f_y = carve(TMP, 2048, [2, EMB])
        f_out = WoT[:, :, :]

        SCORE_AT = [(2, 384), (3, 0), (2, 0), (1, 0)]
        SHIFTED_AT = [(4, 0), (5, 0), (6, 0), (5, 384)]
        PROB_AT = [0, 512, 1024, 896]
        MASKED_AT = [0, 128, 384, 768]

        PS = ctx.enter_context(nc.psum_tensor("PS", [P, 8, 512], f32))

        def bank(n):
            return PS[:, n, :]

        def bank16(n):
            return PS[:, n, :].bitcast(f16)

        def by_head(ap):
            return ap.rearrange("p (h c) -> p h c", c=HD)

        tally = sem("tally")
        consts_ready = sem("consts_ready")
        wdkv_in = sem("wdkv_in")
        heads_in = sem("heads_in")
        vecs_in = sem("vecs_in")
        blockdiag_in = sem("blockdiag_in")
        wo_in = sem("wo_in")
        rows_in = sem("rows_in")
        setup_pe = sem("setup_pe")
        setup_dve = sem("setup_dve")
        setup_act = sem("setup_act")
        setup_chain = sem("setup_chain")
        p_x_in = [sem("p_x_in_even"), sem("p_x_in_odd")]
        p_stats_chain = sem("p_stats_chain")
        p_stats = sem("p_stats")
        p_pool_chain = sem("p_pool_chain")
        p_rstd = sem("p_rstd")
        p_ln_ready = sem("p_ln_ready")
        p_hi_ready = sem("p_hi_ready")
        p_lo_ready = sem("p_lo_ready")
        p_T_done = sem("p_T_done")
        p_xT_ready = sem("p_xT_ready")
        p_G_done = sem("p_G_done")
        p_MN_done = sem("p_MN_done")
        p_prod_ready = sem("p_prod_ready")
        p_var_done = sem("p_var_done")
        p_var_eps = sem("p_var_eps")
        p_root_ready = sem("p_root_ready")
        p_newton_chain = sem("p_newton_chain")
        p_key_raw = sem("p_key_raw")
        p_key_ready = sem("p_key_ready")
        p_khi_ready = sem("p_khi_ready")
        p_klo_ready = sem("p_klo_ready")
        p_value_ready = sem("p_value_ready")
        p_dup_ready = sem("p_dup_ready")
        projected = sem("projected")
        att_consts = sem("att_consts")
        key_rows = sem("key_rows")
        att_mask = sem("att_mask")
        stack_T = sem("stack_T")
        stack_ready = sem("stack_ready")
        scores_done = sem("scores_done")
        max_done = sem("max_done")
        negmax_chain = sem("negmax_chain")
        negmax_ready = sem("negmax_ready")
        negmax_T = sem("negmax_T")
        negmax_stacked = sem("negmax_stacked")
        shifted_done = sem("shifted_done")
        prob_ready = sem("prob_ready")
        pv_done = sem("pv_done")
        rsum_ready = sem("rsum_ready")
        o_stored = sem("o_stored")
        attended = sem("attended")
        o_x_in = [sem("o_x_in_even"), sem("o_x_in_odd")]
        o_staged = sem("o_staged")
        o_T_done = sem("o_T_done")
        o_T_ready = sem("o_T_ready")
        o_proj_done = sem("o_proj_done")
        o_y_chain = sem("o_y_chain")
        o_y_stats = sem("o_y_stats")
        o_y_pool = sem("o_y_pool")
        o_y_rstd = sem("o_y_rstd")
        o_y_ln = sem("o_y_ln")
        o_x1_chain = sem("o_x1_chain")
        o_x1_stats = sem("o_x1_stats")
        o_x1_pool = sem("o_x1_pool")
        o_x1_rstd = sem("o_x1_rstd")
        o_x2_ready = sem("o_x2_ready")
        o_hi_ready = sem("o_hi_ready")
        o_lo_ready = sem("o_lo_ready")
        o_x2T_done = sem("o_x2T_done")
        o_x2T_ready = sem("o_x2T_ready")
        wffn_in = sem("wffn_in")
        mixed = sem("mixed")
        gate_done = sem("gate_done")
        up_done = sem("up_done")
        silu_ready = sem("silu_ready")
        fuse_ready = sem("fuse_ready")
        fhi_ready = sem("fhi_ready")
        flo_ready = sem("flo_ready")
        down_done = sem("down_done")
        y_read = sem("y_read")
        y_chain = sem("y_chain")
        y_stats = sem("y_stats")
        y_pool = sem("y_pool")
        y_rstd = sem("y_rstd")
        y_ln = sem("y_ln")
        out_ready = sem("out_ready")
        chunk_stored = sem("chunk_stored")
        out_stored = sem("out_stored")
        PRIMED = 2

        w_gate, w_up, w_down = (w.bitcast(mybir.dt.int8) for w in (w_gate, w_up, w_down))
        x_tiles = x.rearrange("b (s p) e -> p (b s) e", p=P)
        out_tiles = out.rearrange("b (s p) e -> p (b s) e", p=P)

        def heads_of(t, stack, lo, hi):
            return stack[:, bass.ds(t.batch * HEADS, HEADS), t.sub, lo:hi]

        def arrived(eng, sems, t):
            eng.wait_ge(sems[t.parity], half(t))

        def half(t):
            whole = 16 * (t.const // 2 + 1)
            return whole if t.loop is None else t.loop * (8 * t.unit) + whole

        def across(r):
            return r.unsqueeze(2).to_broadcast([P, HEADS, HD])

        block = ctx.enter_context(nc.Block())

        @block.sync
        def _(sp):
            sp.dma_start(by_head(wdkv_sb), Wdkv.rearrange("h l d -> l h d")).then_inc(wdkv_in, 16)
            sp.dma_start(by_head(wuk_sb), Wuk.rearrange("h l d -> l h d")).then_inc(heads_in, 16)
            sp.dma_start(by_head(wuv_sb), Wuv.rearrange("h l d -> l h d")).then_inc(heads_in, 16)
            for n, v in enumerate((ln_g, ln_b, s_gate.rearrange("(c p) -> c p", p=P),
                                   s_up.rearrange("(c p) -> c p", p=P))):
                sp.dma_start(vec_rows[16 * n:16 * n + 16, :], v).then_inc(vecs_in, 16)
            sp.wait_ge(setup_dve, nth(SETUP_DVE, "bdzero"))
            for a in range(GH):
                for dst, w in ((bdq, Wq), (bdo, Wo_h)):
                    sp.dma_start(dst[HD * a:HD * a + HD, :, HD * a:HD * a + HD],
                                 w.rearrange("(g a) i j -> a i g j", a=GH)[a]).then_inc(blockdiag_in, 16)
            sp.dma_start(wo_nat, Wo.rearrange("(m p) n -> p m n", p=P)).then_inc(wo_in, 16)
            sp.dma_start(bo_all[:, :], bo.partition_broadcast(P)).then_inc(rows_in, 16)
            sp.dma_start(sdown[:, :], s_down.partition_broadcast(P)).then_inc(rows_in, 16)

            def load_x(dst, sems, used, t):
                wait(sp, used, t.times(1, -1))
                sp.dma_start(dst[:, t.parity, :], x_tiles[:, bass.ds(t.times(1), 1), :]
                             .rearrange("p a e -> p (a e)")).then_inc(sems[t.parity], 16)

            pipelined(sp, TILES, 4, [(0, lambda t: load_x(p_x, p_x_in, p_ln_ready, t))])
            sp.wait_ge(attended, 3)
            pipelined(sp, TILES, 4, [(0, lambda t: load_x(o_x, o_x_in, o_x1_stats, t))])
            sp.sem_inc(chunk_stored, 1)
            with sp.Fori(0, BATCH) as c:
                for u in range(CTILES):
                    sp.wait_ge(out_ready, c * CTILES + (u + 2))
                    sp.dma_start(out_tiles[:, bass.ds(c * CTILES + u, 1), :].rearrange("p a e -> p (a e)"),
                                 f_out[:, u, :]).then_inc(out_stored, 16)
                sp.wait_ge(out_stored, (c + 1) * (16 * CTILES))
                sp.sem_inc(chunk_stored, 1)
            sp.wait_ge(out_stored, 16 * TILES)

        @block.gpsimd
        def _(pool):
            for m, v in ((ident, 0.0), (ident16, 0.0), (identb, 0.0), (causalT, 0.0), (halfneg, -0.5)):
                pool.memset(m[:, :], v).then_inc(consts_ready, 1)
            pool.wait_ge(consts_ready, 5)
            for m in (ident, ident16, identb):
                pool.affine_select(out=m[:, :], in_=m[:, :], compare_op=ALU.not_equal, fill=1.0, base=0,
                                   pattern=[[-1, P]], channel_multiplier=1).then_inc(consts_ready, 1)
            pool.affine_select(out=causalT[:, :], in_=causalT[:, :], compare_op=ALU.is_ge, fill=NEG, base=0,
                               pattern=[[1, P]], channel_multiplier=-1).then_inc(consts_ready, 1)

            def rstd(st, stats, used, chain, done, t, gain=None):
                links = 2 if gain is None else 3
                pool.wait_ge(stats, t.times(1, 1))
                wait_apart(pool, used, t.times(1, -1), tally)
                pool.tensor_scalar(st[:, 8:9], st[:, 7:8], EPS, None, ALU.add).then_inc(chain, 1)
                pool.wait_ge(chain, t.times(links, 1))
                pool.tensor_tensor(st[:, 9:10], st[:, 8:9], halfneg[:, :], ALU.pow).then_inc(chain, 1)
                wait_apart(pool, chain, t.times(links, 2), tally)
                if gain is not None:
                    pool.tensor_scalar(st[:, 9:10], st[:, 9:10], gain, None, ALU.mult).then_inc(chain, 1)
                    wait_apart(pool, chain, t.times(links, 3), tally)
                pool.tensor_scalar(st[:, 10:11], st[:, 6:7], st[:, 9:10], -1.0, ALU.mult, ALU.mult)\
                    .then_inc(done, 1)

            def x_scale(t):
                rstd(small[:, t.parity, :], p_stats, p_ln_ready, p_pool_chain, p_rstd, t)

            def x_low(t):
                pool.wait_ge(p_hi_ready, t.times(1, 1))
                pool.tensor_tensor(heads_of(t, qst, HD, 2 * HD), by_head(p_ln[:, t.parity, :]),
                                   heads_of(t, qst, 0, HD), ALU.subtract).then_inc(p_lo_ready, 1)

            def key_bias(t):
                pool.wait_ge(p_key_raw, t.times(1, 1))
                pool.tensor_tensor(p_key[:, t.parity, :], p_key[:, t.parity, :], keybias[:, :], ALU.add)\
                    .then_inc(p_key_ready, 1)

            pool.wait_ge(consts_ready, 9)
            pipelined(pool, TILES, 4, [(0, x_scale), (0, x_low), (2, key_bias)])
            pool.wait_ge(p_lo_ready, TILES)
            pool.wait_ge(p_key_ready, TILES)
            pool.sem_inc(projected, 1)

            pool.wait_ge(projected, 4)
            pool.memset(causal, 0.0).then_inc(att_consts, 1)
            pool.wait_ge(att_consts, 1)
            pool.affine_select(out=causal[:, SEQ - P:], in_=causal[:, SEQ - P:], compare_op=ALU.is_ge, fill=NEG,
                               base=0, pattern=[[-1, P]], channel_multiplier=1).then_inc(att_mask, 1)

            pool.wait_ge(attended, 3)
            for m, w in enumerate((w_gate, w_up)):
                pool.dma_start(w_gu[:, m, :, :], w.rearrange("(k p) n -> p k n", p=P)).then_inc(wffn_in, 16)
            pool.dma_start(w_dn, w_down.rearrange("(i p) n -> p i n", p=P)).then_inc(wffn_in, 16)

            def y_scale(t):
                rstd(small[:, t.parity, :], o_y_stats, o_y_ln, o_y_pool, o_y_rstd, t)

            def x1_scale(t):
                rstd(small[:, t.parity, 32:], o_x1_stats, o_x2_ready, o_x1_pool, o_x1_rstd, t, gain=X2_SCALE)

            def x2_low(t):
                pool.wait_ge(o_hi_ready, t.times(1, 1))
                pool.tensor_tensor(o_parts[:, t.parity, 1, :], o_x2, o_parts[:, t.parity, 0, :], ALU.subtract)\
                    .then_inc(o_lo_ready, 1)

            pipelined(pool, TILES, 4, [(2, x1_scale), (1, y_scale), (2, x2_low)])
            pool.wait_ge(o_lo_ready, TILES)
            pool.sem_inc(mixed, 1)

            pool.wait_ge(mixed, 4)
            pool.sem_inc(flo_ready, PRIMED)
            with pool.Fori(0, BATCH) as c:
                with pool.Fori(0, ITILES // 2) as j:
                    for u in range(2):
                        i = j * 2 + u
                        pool.wait_ge(fhi_ready, c * ITILES + i + (1 + PRIMED))
                        pool.tensor_tensor(fused[:, 1, bass.ds(i, 1), :].rearrange("p a t -> p (a t)"),
                                           f_prod[:, u, :],
                                           fused[:, 0, bass.ds(i, 1), :].rearrange("p a t -> p (a t)"),
                                           ALU.subtract).then_inc(flo_ready, 1)
                for u in range(CTILES):
                    t = c * CTILES + u
                    st = small[:, u % 2, :]
                    wait_apart(pool, y_stats, t + 1, tally)
                    pool.tensor_scalar(st[:, 8:9], st[:, 7:8], EPS, None, ALU.add).then_inc(y_pool, 1)
                    pool.wait_ge(y_pool, t * 2 + 1)
                    pool.wait_ge(y_ln, t + 1)
                    pool.tensor_tensor(st[:, 9:10], st[:, 8:9], halfneg[:, :], ALU.pow).then_inc(y_pool, 1)
                    wait_apart(pool, y_pool, t * 2 + 2, tally)
                    pool.tensor_scalar(st[:, 10:11], st[:, 6:7], st[:, 9:10], -1.0, ALU.mult, ALU.mult)\
                        .then_inc(y_rstd, 1)

        @block.scalar
        def _(act):
            for name, n, dst in (("wuvT", 2, wuvT), ("bdoT", 4, bdoT)):
                act.wait_ge(setup_pe, nth(SETUP_PE, name))
                act.activation(dst.rearrange("p g c -> p (g c)"), bank(n), ACT.Copy).then_inc(setup_act, 1)
            for k in range(GROUPS):
                act.wait_ge(setup_pe, nth(SETUP_PE, f"woT{k}"))
                act.activation(WoT[:, k, :], bank(6 + k % 2), ACT.Copy).then_inc(setup_act, 1)

            def ln(t):
                st = small[:, t.parity, :]
                act.wait_ge(p_rstd, t.times(1, 1))
                wait(act, p_lo_ready, t.times(1, -1))
                wait(act, p_T_done, t.times(1, -1))
                act.activation(p_ln[:, t.parity, :], p_x[:, t.parity, :], ACT.Identity,
                               scale=st[:, 9:10], bias=st[:, 10:11]).then_inc(p_ln_ready, 1)
                act.wait_ge(p_ln_ready, t.times(1, 1))
                act.activation(heads_of(t, qst, 0, HD), by_head(p_ln[:, t.parity, :]), ACT.Copy)\
                    .then_inc(p_hi_ready, 1)

            def xT(t):
                act.wait_ge(p_T_done, t.times(1, 1))
                wait(act, p_prod_ready, t.times(1, -1))
                wait(act, p_MN_done, t.times(1, -1))
                act.activation(p_xT[:, t.parity, :, :].rearrange("p g c -> p (g c)"), bank(0), ACT.Copy)\
                    .then_inc(p_xT_ready, 1)

            def root(t):
                st = small[:, t.parity, 16:]
                act.wait_ge(p_var_eps, t.times(1, 1))
                act.activation(st[:, 16:32], st[:, 0:16], ACT.Sqrt).then_inc(p_root_ready, 1)

            def key_high(t):
                act.wait_ge(p_key_ready, t.times(1, 1))
                act.activation(heads_of(t, kst, 0, HD), by_head(p_key[:, t.parity, :]), ACT.Copy)\
                    .then_inc(p_khi_ready, 1)

            pipelined(act, TILES, 4, [(0, ln), (0, xT), (1, root), (2, key_high)])
            act.wait_ge(p_khi_ready, TILES)
            act.wait_ge(p_xT_ready, TILES)
            act.sem_inc(projected, 1)

            def stacks(h):
                act.wait_ge(stack_T, h.times(1, 1))
                wait(act, shifted_done, h.times(1, -1))
                act.activation(qk[0:STACK, h.parity, :, :].rearrange("p a t -> p (a t)"),
                               bank16(0)[0:STACK, :], ACT.Copy).then_inc(stack_ready, 1)

            def exps(h):
                act.wait_ge(shifted_done, h.times(1, 1))
                wait(act, pv_done, h.times(1, -1))
                act.activation(prob[:, h.parity, 0:1024], PS[:, 4:6, :].rearrange("p a t -> p (a t)"), ACT.Exp,
                               scale=kscale[:, 2:3])
                act.activation(prob[:, h.parity, 1024:1280], PS[:, 6, 0:256], ACT.Exp,
                               scale=kscale[:, 2:3]).then_inc(prob_ready, 1)

            act.wait_ge(projected, 4)
            pipelined(act, UNITS, 2, [(2, exps), (0, stacks)])
            act.wait_ge(stack_ready, UNITS)
            act.wait_ge(prob_ready, UNITS)
            act.sem_inc(attended, 1)

            def stage_o(t):
                wait(act, o_T_done, t.times(1, -1))
                act.activation(by_head(o_in[:, t.parity, :]), heads_of(t, ost, 0, HD), ACT.Copy)\
                    .then_inc(o_staged, 1)

            def oT(t):
                act.wait_ge(o_T_done, t.times(1, 1))
                wait(act, o_proj_done, t.times(1, -1))
                act.activation(o_T[:, t.parity, :, :].rearrange("p g c -> p (g c)"), bank(0), ACT.Copy)\
                    .then_inc(o_T_ready, 1)

            def y_norm(t):
                st = small[:, t.parity, :]
                act.wait_ge(o_y_rstd, t.times(1, 1))
                act.activation(o_y[:, t.parity, :], o_y[:, t.parity, :], ACT.Identity,
                               scale=st[:, 9:10], bias=st[:, 10:11]).then_inc(o_y_ln, 1)

            def x2_high(t):
                act.wait_ge(o_x2_ready, t.times(1, 1))
                wait(act, o_x2T_done, t.times(1, -1))
                act.activation(o_parts[:, t.parity, 0, :], o_x2, ACT.Copy).then_inc(o_hi_ready, 1)

            def x2_T(t):
                act.wait_ge(o_x2T_done, t.times(1, 1))
                act.activation(x2T[:, :, bass.ds(t.times(P), P)],
                               bank16(3).rearrange("p (k c) -> p k c", c=P), ACT.Copy).then_inc(o_x2T_ready, 1)

            act.wait_ge(attended, 3)
            pipelined(act, TILES, 4, [(0, stage_o), (0, oT), (1, y_norm), (2, x2_high), (3, x2_T)])
            act.wait_ge(o_x2T_ready, TILES)
            act.sem_inc(mixed, 1)

            act.wait_ge(mixed, 4)
            for primed in (silu_ready, fhi_ready, y_ln):
                act.sem_inc(primed, PRIMED)
            with act.Fori(0, BATCH) as c:
                act.wait_ge(down_done, c * CTILES + 1)
                with act.Fori(0, ITILES // 2) as j:
                    for u in range(2):
                        i = j * 2 + u
                        act.wait_ge(gate_done, c * ITILES + i + 1)
                        act.wait_ge(fuse_ready, c * ITILES + i + 1)
                        act.activation(f_silu[:, u, :], bank(u), ACT.Silu, scale=sgate[:, bass.ds(i, 1)])\
                            .then_inc(silu_ready, 1)
                        act.wait_ge(fuse_ready, c * ITILES + i + (1 + PRIMED))
                        act.activation(fused[:, 0, bass.ds(i, 1), :].rearrange("p a t -> p (a t)"),
                                       f_prod[:, u, :], ACT.Copy).then_inc(fhi_ready, 1)
                for u in range(CTILES):
                    st = small[:, u % 2, :]
                    act.wait_ge(y_rstd, c * CTILES + (u + 1))
                    act.activation(f_y[:, u % 2, :], f_y[:, u % 2, :], ACT.Identity,
                                   scale=st[:, 9:10], bias=st[:, 10:11]).then_inc(y_ln, 1)

        @block.vector
        def _(dve):
            links = [0]

            def link(ins):
                links[0] += 1
                ins.then_inc(setup_chain, 1)
                dve.wait_ge(setup_chain, links[0])

            def absolute(out, a):
                return dve.scalar_tensor_tensor(out, a, -1.0, a, ALU.mult, ALU.max)

            dve.memset(ones[:, :], 1.0).then_inc(setup_dve, 1)
            dve.memset(bdq, 0.0)
            dve.memset(bdo, 0.0).then_inc(setup_dve, 1)
            dve.memset(GMN[:, :, :, :], 0.0).then_inc(setup_dve, 1)
            dve.memset(negmax[:, :, :, :], 0.0)
            link(dve.memset(headsum[:, :], 0.0))
            for a in range(GH):
                dve.memset(headsum[HD * a:HD * a + HD, a:a + 1], 1.0)

            dve.wait_ge(wdkv_in, 16)
            dve.wait_ge(setup_pe, nth(SETUP_PE, "mean"))
            dve.scalar_tensor_tensor(wc, bank(0), -1.0 / LAT, wdkv_sb, ALU.mult, ALU.add).then_inc(setup_dve, 1)
            for name, n, dst in (("wukT", 1, wukT.rearrange("p g c -> p (g c)")), ("vecT", 5, vec[:, :]),
                                 ("bdqT", 3, bdqT.rearrange("p g c -> p (g c)"))):
                dve.wait_ge(setup_pe, nth(SETUP_PE, name))
                dve.tensor_copy(dst, PS[:, n, 0:dst.shape[1]]).then_inc(setup_dve, 1)
            dve.wait_ge(setup_dve, nth(SETUP_DVE, "vecT"))
            g, b = vec[:, 0:HEADS], vec[:, HEADS:2 * HEADS]
            absolute(scratch[:, 0:16], g)
            link(absolute(scratch[:, 16:32], b))
            link(dve.scalar_tensor_tensor(scratch[:, 32:48], scratch[:, 0:16], LATENT_MAX, scratch[:, 16:32],
                                          ALU.mult, ALU.add))
            dve.wait_ge(setup_pe, nth(SETUP_PE, "A"))
            dve.tensor_tensor(by_head(gA), by_head(bank(6)), across(g), ALU.mult).then_inc(setup_dve, 1)
            dve.tensor_tensor(by_head(bA), by_head(bank(6)), across(b), ALU.mult).then_inc(setup_dve, 1)
            link(dve.tensor_tensor(by_head(absA), by_head(bank(6)), across(scratch[:, 32:48]), ALU.mult))
            absolute(absA, absA).then_inc(setup_dve, 1)
            dve.wait_ge(setup_pe, nth(SETUP_PE, "U"))
            dve.tensor_tensor(by_head(gU), by_head(bank(7)), across(g), ALU.mult).then_inc(setup_dve, 1)
            dve.tensor_tensor(by_head(bU), by_head(bank(7)), across(b), ALU.mult).then_inc(setup_dve, 1)

            dve.wait_ge(setup_pe, nth(SETUP_PE, "keybound"))
            link(dve.tensor_reduce(kscale[:, 0:1], bank(3), AX.X, ALU.max))
            link(dve.tensor_scalar(kscale[:, 0:1], kscale[:, 0:1], 1e-30, 1.0 / KEY_BOUND, ALU.max, ALU.mult))
            link(dve.reciprocal(kscale[:, 1:2], kscale[:, 0:1]))
            dve.tensor_scalar(kscale[:, 2:3], kscale[:, 0:1], 1.0 / math.sqrt(LAT), None, ALU.mult)
            for m, name in enumerate(("G", "M", "N")):
                dve.wait_ge(setup_pe, nth(SETUP_PE, name))
                for a in range(GH):
                    rows = slice(HD * a, HD * a + HD)
                    src = bank(m).rearrange("p (g c) -> p g c", c=P)[rows, :, rows]
                    last = dve.tensor_scalar(GMN[rows, :, m, rows], src,
                                             (1.0 / LAT, kscale[rows, 1:2], 1.0)[m], None, ALU.mult)
                last.then_inc(setup_dve, 1)
            dve.wait_ge(setup_pe, nth(SETUP_PE, "keybias"))
            dve.tensor_scalar(keybias[:, :], bank(4), kscale[:, 1:2], None, ALU.mult).then_inc(setup_dve, 1)
            dve.wait_ge(setup_pe, nth(SETUP_PE, "vb"))
            dve.tensor_copy(vb_sb.rearrange("p g c -> p (g c)"), bank(5)).then_inc(setup_dve, 1)

            link(dve.tensor_tensor(scratch[:, 0:16], vec[:, 32:48], vec[:, 48:64], ALU.mult))
            link(absolute(scratch[:, 0:16], scratch[:, 0:16]))
            dve.tensor_reduce(scratch[:, 16:17], scratch[:, 0:16], AX.X, ALU.max).then_inc(setup_dve, 1)
            dve.wait_ge(setup_pe, nth(SETUP_PE, "fuseT"))
            dve.tensor_reduce(scratch[0:1, 17:18], bank(3)[0:1, 0:P], AX.X, ALU.max).then_inc(setup_dve, 1)
            dve.wait_ge(setup_pe, nth(SETUP_PE, "fuseall"))
            link(dve.tensor_scalar(scratch[:, 18:19], bank(3)[:, 0:1], 1e-30, RAW_BOUND ** 2 / FUSE_BOUND,
                                   ALU.max, ALU.mult))
            link(dve.reciprocal(scratch[:, 19:20], scratch[:, 18:19]))
            dve.tensor_scalar(sgate[:, :], vec[:, 32:48], 1.0 / X2_SCALE, None, ALU.mult)
            dve.tensor_scalar(sup[:, :], vec[:, 48:64], scratch[:, 19:20], 1.0 / X2_SCALE, ALU.mult, ALU.mult)
            dve.wait_ge(rows_in, 32)
            dve.tensor_scalar(sdown[:, :], sdown[:, :], scratch[:, 18:19], None, ALU.mult).then_inc(setup_dve, 1)
            dve.wait_ge(setup_pe, nth(SETUP_PE, "bo"))
            dve.tensor_tensor(bo_all[:, :], bank(5), bo_all[:, :], ALU.add).then_inc(setup_dve, 1)
            dve.memset(vst[:, :, :, HD:VW], 1.0).then_inc(setup_dve, 1)

            def x_stats(t):
                st = small[:, t.parity, :]
                arrived(dve, p_x_in, t)
                wait(dve, p_rstd, t.times(1, -1))
                dve.bn_stats(st[:, 0:6], p_x[:, t.parity, :]).then_inc(p_stats_chain, 1)
                wait_apart(dve, p_stats_chain, t.times(1, 1), tally)
                dve.bn_aggr(st[:, 6:8], st[:, 0:6]).then_inc(p_stats, 1)

            def product(t):
                dve.wait_ge(p_G_done, t.times(1, 1))
                wait(dve, p_var_done, t.times(1, 0))
                dve.tensor_tensor(p_prod.rearrange("p g c -> p (g c)"), bank(1),
                                  p_xT[:, t.parity, :, :].rearrange("p g c -> p (g c)"), ALU.mult)\
                    .then_inc(p_prod_ready, 1)

            def newton(t):
                st = small[:, t.parity, 16:]
                a, y, s = st[:, 0:16], st[:, 32:48], st[:, 48:64]
                dve.wait_ge(p_root_ready, t.times(1, 1))
                dve.reciprocal(y, st[:, 16:32]).then_inc(p_newton_chain, 1)
                dve.wait_ge(p_newton_chain, t.times(5, 1))
                dve.tensor_tensor(s, y, y, ALU.mult).then_inc(p_newton_chain, 1)
                dve.wait_ge(p_newton_chain, t.times(5, 2))
                dve.tensor_tensor(s, s, a, ALU.mult).then_inc(p_newton_chain, 1)
                dve.wait_ge(p_newton_chain, t.times(5, 3))
                dve.tensor_scalar(s, s, -0.5, 1.5, ALU.mult, ALU.add).then_inc(p_newton_chain, 1)
                dve.wait_ge(p_newton_chain, t.times(5, 4))
                dve.tensor_tensor(y, y, s, ALU.mult).then_inc(p_newton_chain, 1)

            def key_raw(t):
                dve.wait_ge(p_newton_chain, t.times(5, 5))
                dve.wait_ge(p_MN_done, t.times(1, 1))
                wait(dve, p_khi_ready, t.times(1, -1))
                dve.tensor_tensor(by_head(p_key[:, t.parity, :]), by_head(bank(4 + t.parity)),
                                  across(small[:, t.parity, 48:64]), ALU.mult).then_inc(p_key_raw, 1)

            def var_eps(t):
                dve.wait_ge(p_var_done, t.times(1, 1))
                dve.tensor_scalar(small[:, t.parity, 16:32], bank(3)[:, 0:HEADS], 0.0, EPS, ALU.max, ALU.add)\
                    .then_inc(p_var_eps, 1)

            def value(t):
                dve.tensor_tensor(heads_of(t, vst, 0, HD), by_head(bank(6 + t.parity)),
                                  across(small[:, t.parity, 48:64]), ALU.mult).then_inc(p_value_ready, 1)

            def parts(t):
                dve.wait_ge(p_hi_ready, t.times(1, 1))
                dve.tensor_copy(heads_of(t, qst, 2 * HD, STACK), heads_of(t, qst, 0, HD))
                dve.wait_ge(p_khi_ready, t.times(1, 1))
                dve.tensor_copy(heads_of(t, kst, HD, 2 * HD), heads_of(t, kst, 0, HD))
                dve.tensor_tensor(heads_of(t, kst, 2 * HD, STACK), by_head(p_key[:, t.parity, :]),
                                  heads_of(t, kst, 0, HD), ALU.subtract).then_inc(p_klo_ready, 1)

            pipelined(dve, TILES, 4, [(0, x_stats), (1, product), (2, newton), (2, key_raw), (1, var_eps),
                                      (2, value), (2, parts)])
            dve.wait_ge(p_klo_ready, TILES)
            dve.sem_inc(projected, 1)

            dve.wait_ge(projected, 4)
            dve.memset(qk[STACK:P, :, 1, :], 0.0).then_inc(key_rows, 1)
            dve.wait_ge(key_rows, 1)
            dve.memset(qk[STACK:STACK + 2, :, 1, :], 1.0).then_inc(key_rows, 1)
            dve.wait_ge(att_mask, 1)

            def maxima(h):
                wait_apart(dve, scores_done, h.times(1, 1), tally)
                for s, (n, at) in enumerate(SCORE_AT):
                    width = (s + 1) * P
                    last = dve.tensor_tensor_reduce(
                        out=masked[:, MASKED_AT[s]:MASKED_AT[s] + width], in0=PS[:, n, at:at + width], in1=causal[:, SEQ - width:],
                        scale=1.0, scalar=NEG, op0=ALU.add, op1=ALU.max,
                        accum_out=rowmax[:, h.parity, s:s + 1])
                last.then_inc(max_done, 1)
                dve.wait_ge(max_done, h.times(1, 1))
                wait(dve, negmax_T, h.times(1, -1))
                dve.tensor_scalar(negmax[:, h.parity, :, 0], rowmax[:, h.parity, :], -1.0, None, ALU.mult)\
                    .then_inc(negmax_chain, 1)
                dve.wait_ge(negmax_chain, h.times(1, 1))
                dve.scalar_tensor_tensor(negmax[:, h.parity, :, 1], rowmax[:, h.parity, :], -1.0,
                                         negmax[:, h.parity, :, 0], ALU.mult, ALU.subtract)\
                    .then_inc(negmax_ready, 1)

            def negmax_rows(h):
                dve.wait_ge(negmax_T, h.times(1, 1))
                wait(dve, shifted_done, h.times(1, -1))
                dve.tensor_copy(qk[STACK:P, h.parity, 0, :], bank16(0)[STACK:P, 0:SEQ])\
                    .then_inc(negmax_stacked, 1)

            def normalise(h):
                dve.wait_ge(pv_done, h.times(1, 1))
                pv = PS[:, 7, 0:SEQ_TILES * VW].rearrange("p (s c) -> p s c", c=VW)
                dve.reciprocal(rsum[:, :], pv[:, :, HD]).then_inc(rsum_ready, 1)
                dve.wait_ge(rsum_ready, h.times(1, 1))
                dve.tensor_tensor(ost[:, bass.ds(h.times(1), 1), :, :].rearrange("p a s c -> p (a s) c"),
                                  pv[:, :, 0:HD],
                                  rsum[:, :].unsqueeze(2).to_broadcast([P, SEQ_TILES, HD]), ALU.mult)\
                    .then_inc(o_stored, 1)

            pipelined(dve, UNITS, 2, [(1, maxima), (3, normalise), (1, negmax_rows)])
            dve.wait_ge(o_stored, UNITS)
            dve.sem_inc(attended, 1)

            def x1(t):
                st = small[:, t.parity, 32:]
                arrived(dve, o_x_in, t)
                dve.wait_ge(o_y_ln, t.times(1, 1))
                wait(dve, o_x1_rstd, t.times(1, -1))
                dve.tensor_tensor(heads_of(t, ost, 0, HD), by_head(o_y[:, t.parity, :]),
                                  by_head(o_x[:, t.parity, :]), ALU.add).then_inc(o_x1_chain, 1)
                wait_apart(dve, o_x1_chain, t.times(2, 1), tally)
                dve.bn_stats(st[:, 0:6], heads_of(t, ost, 0, HD)).then_inc(o_x1_chain, 1)
                wait_apart(dve, o_x1_chain, t.times(2, 2), tally)
                dve.bn_aggr(st[:, 6:8], st[:, 0:6]).then_inc(o_x1_stats, 1)

            def y(t):
                st = small[:, t.parity, :]
                dve.wait_ge(o_proj_done, t.times(1, 1))
                wait(dve, o_y_rstd, t.times(1, -1))
                dve.tensor_tensor(o_y[:, t.parity, :], bank(1 + t.parity), bo_all[:, :], ALU.add)\
                    .then_inc(o_y_chain, 1)
                dve.wait_ge(o_y_chain, t.times(2, 1))
                dve.bn_stats(st[:, 0:6], o_y[:, t.parity, :]).then_inc(o_y_chain, 1)
                wait_apart(dve, o_y_chain, t.times(2, 2), tally)
                dve.bn_aggr(st[:, 6:8], st[:, 0:6]).then_inc(o_y_stats, 1)

            def x2(t):
                st = small[:, t.parity, 32:]
                dve.wait_ge(o_x1_rstd, t.times(1, 1))
                wait(dve, o_lo_ready, t.times(1, 0))
                dve.tensor_scalar(by_head(o_x2), heads_of(t, ost, 0, HD), st[:, 9:10], st[:, 10:11],
                                  ALU.mult, ALU.add).then_inc(o_x2_ready, 1)

            dve.wait_ge(attended, 3)
            pipelined(dve, TILES, 4, [(2, x1), (1, y), (2, x2)])
            dve.wait_ge(o_x2_ready, TILES)
            dve.sem_inc(mixed, 1)

            dve.wait_ge(mixed, 4)
            dve.sem_inc(fuse_ready, PRIMED)
            dve.sem_inc(y_read, PRIMED)
            dve.sem_inc(out_ready, 1)
            with dve.Fori(0, BATCH) as c:
                with dve.Fori(0, ITILES // 2) as j:
                    for u in range(2):
                        i = j * 2 + u
                        n = c * ITILES + i
                        dve.wait_ge(up_done, n + 1)
                        dve.wait_ge(silu_ready, n + (1 + PRIMED))
                        dve.wait_ge(flo_ready, n + 1)
                        dve.scalar_tensor_tensor(f_prod[:, u, :], bank(2 + u), sup[:, bass.ds(i, 1)],
                                                 f_silu[:, u, :], ALU.mult, ALU.mult).then_inc(fuse_ready, 1)

                def add_residual(u):
                    t = c * CTILES + u
                    dve.wait_ge(y_ln, t + (1 + PRIMED))
                    dve.tensor_tensor(by_head(f_out[:, u, :]), by_head(f_y[:, u % 2, :]),
                                      ost[:, bass.ds(c * HEADS, HEADS), u, :], ALU.add).then_inc(out_ready, 1)

                dve.wait_ge(chunk_stored, c + 1)
                for u in range(CTILES):
                    t = c * CTILES + u
                    st = small[:, u % 2, :]
                    dve.wait_ge(out_ready, c * CTILES + (max(u - 1, 0) + 1))
                    dve.wait_ge(down_done, t + 2)
                    dve.tensor_tensor(f_y[:, u % 2, :], bank(4 + u % 2), sdown[:, :], ALU.mult)\
                        .then_inc(y_read, 1)
                    dve.wait_ge(y_read, t + (1 + PRIMED))
                    dve.bn_stats(st[:, 0:6], f_y[:, u % 2, :]).then_inc(y_chain, 1)
                    wait_apart(dve, y_chain, t + 1, tally)
                    dve.bn_aggr(st[:, 6:8], st[:, 0:6]).then_inc(y_stats, 1)
                    if u:
                        add_residual(u - 1)
                add_residual(CTILES - 1)

        @block.tensor
        def _(pe):
            def transposes(n, src, ident_, name):
                for g in range(GROUPS):
                    last = pe.transpose(PS[:, n, P * g:P * g + P], src(g), ident_)
                last.then_inc(setup_pe, 1)

            def products(n, lhs, rhs, name):
                for g in range(GROUPS):
                    last = pe.matmul(PS[:, n, P * g:P * g + P], lhs(g), rhs(g), start=True, stop=True)
                last.then_inc(setup_pe, 1)

            def tile_of(m):
                return lambda g: m[:, P * g:P * g + P]

            def group_of(m):
                return lambda g: m[:, g, :]

            pe.wait_ge(setup_dve, nth(SETUP_DVE, "ones"))
            pe.wait_ge(wdkv_in, 16)
            pe.matmul(bank(0), ones[:, :], wdkv_sb, start=True, stop=True).then_inc(setup_pe, 1)
            pe.wait_ge(consts_ready, 9)
            pe.wait_ge(heads_in, 32)
            transposes(1, tile_of(wuk_sb), ident[:, :], "wukT")
            transposes(2, tile_of(wuv_sb), ident[:, :], "wuvT")
            pe.wait_ge(vecs_in, 64)
            pe.transpose(PS[:, 5, 0:64], vec_rows[0:64, :], ident[0:64, 0:64]).then_inc(setup_pe, 1)
            pe.wait_ge(blockdiag_in, 128)
            transposes(3, group_of(bdq), ident[:, :], "bdqT")
            transposes(4, group_of(bdo), ident[:, :], "bdoT")
            pe.wait_ge(setup_dve, nth(SETUP_DVE, "bdqT"))
            products(6, group_of(wukT), group_of(bdqT), "A")
            pe.wait_ge(setup_act, nth(SETUP_ACT, "bdoT"))
            products(7, group_of(wuvT), group_of(bdoT), "U")
            products(0, tile_of(wc), tile_of(wc), "G")
            pe.wait_ge(setup_dve, nth(SETUP_DVE, "gA"))
            products(1, tile_of(wc), tile_of(gA), "M")
            pe.wait_ge(setup_dve, nth(SETUP_DVE, "gU"))
            products(2, tile_of(wc), tile_of(gU), "N")
            pe.wait_ge(setup_dve, nth(SETUP_DVE, "absA"))
            pe.matmul(bank(3), ones[:, :], absA, start=True, stop=True).then_inc(setup_pe, 1)
            pe.matmul(bank(4), ones[:, :], bA, start=True, stop=True).then_inc(setup_pe, 1)
            pe.wait_ge(setup_dve, nth(SETUP_DVE, "bU"))
            products(5, tile_of(bU), lambda g: ones[:, :], "vb")
            pe.wait_ge(wo_in, 16)
            for k in range(GROUPS):
                if k >= 2:
                    pe.wait_ge(setup_act, nth(SETUP_ACT, f"woT{k - 2}"))
                transposes(6 + k % 2, lambda g: wo_nat[:, g, P * k:P * k + P], ident[:, :], f"woT{k}")
            pe.wait_ge(setup_dve, nth(SETUP_DVE, "fusemax"))
            pe.transpose(bank(3)[0:1, 0:P], scratch[:, 16:17], ident[:, :]).then_inc(setup_pe, 1)
            pe.wait_ge(setup_dve, nth(SETUP_DVE, "fusered"))
            pe.matmul(bank(3)[:, 0:1], ones[0:1, :], scratch[0:1, 17:18], start=True, stop=True)\
                .then_inc(setup_pe, 1)
            pe.wait_ge(setup_act, nth(SETUP_ACT, "woT3"))
            for g in range(GROUPS):
                last = pe.matmul(bank(5), vb_sb[:, g, :], WoT[:, g, :], start=(g == 0), stop=(g == GROUPS - 1))
            last.then_inc(setup_pe, 1)

            def keys_values(t):
                wait(pe, p_value_ready, t.times(1, -1))
                for m, n in ((1, 4), (2, 6)):
                    for g in range(GROUPS):
                        last = pe.matmul(PS[:, n + t.parity, P * g:P * g + P], p_xT[:, t.parity, g, :],
                                         GMN[:, g, m, :], start=True, stop=True)
                last.then_inc(p_MN_done, 1)

            def variance(t):
                pe.wait_ge(p_prod_ready, t.times(1, 1))
                wait(pe, p_var_eps, t.times(1, 0))
                for g in range(GROUPS):
                    last = pe.matmul(bank(3)[:, GH * g:GH * g + GH], p_prod[:, g, :], headsum[:, :],
                                     start=True, stop=True)
                last.then_inc(p_var_done, 1)

            def xln_T(t):
                pe.wait_ge(p_ln_ready, t.times(1, 1))
                wait(pe, p_xT_ready, t.times(1, 0))
                for g in range(GROUPS):
                    last = pe.transpose(PS[:, 0, P * g:P * g + P], p_ln[:, t.parity, P * g:P * g + P],
                                        ident[:, :])
                last.then_inc(p_T_done, 1)

            def gram(t):
                pe.wait_ge(p_xT_ready, t.times(1, 1))
                wait(pe, p_prod_ready, t.times(1, 0))
                for g in range(GROUPS):
                    last = pe.matmul(PS[:, 1, P * g:P * g + P], GMN[:, g, 0, :], p_xT[:, t.parity, g, :],
                                     start=True, stop=True)
                last.then_inc(p_G_done, 1)

            pe.wait_ge(setup_dve, nth(SETUP_DVE, "done"))
            pipelined(pe, TILES, 4, [(1, keys_values), (1, variance), (0, xln_T), (0, gram)])
            pe.wait_ge(p_MN_done, TILES)
            pe.wait_ge(p_var_done, TILES)
            pe.sem_inc(projected, 1)

            def scores(h):
                pe.wait_ge(stack_ready, h.times(1, 1))
                wait(pe, max_done, h.times(1, 0))
                for s, (n, at) in enumerate(SCORE_AT):
                    last = pe.matmul(PS[:, n, at:at + (s + 1) * P], qk[0:STACK, h.parity, 0, P * s:P * s + P],
                                     qk[0:STACK, h.parity, 1, 0:(s + 1) * P], start=True, stop=True)
                last.then_inc(scores_done, 1)

            def shifted(h):
                pe.wait_ge(negmax_stacked, h.times(1, 1))
                wait(pe, prob_ready, h.times(1, 0))
                for t, (n, at) in enumerate(SHIFTED_AT):
                    pe.matmul(PS[:, n, at:at + SEQ - P * t], qk[:, h.parity, 1, P * t:P * t + P],
                              qk[:, h.parity, 0, P * t:SEQ], start=True, stop=False)
                    last = pe.matmul(PS[:, n, at:at + P], identb[:, :], causalT[:, :], start=False, stop=True)
                last.then_inc(shifted_done, 1)

            def weighted(h):
                pe.wait_ge(prob_ready, h.times(1, 1))
                wait(pe, o_stored, h.times(1, 0))
                for s in range(SEQ_TILES):
                    for t in range(s + 1):
                        at = PROB_AT[t] + P * (s - t)
                        last = pe.matmul(PS[:, 7, VW * s:VW * s + VW], prob[:, h.parity, at:at + P],
                                         vst[:, bass.ds(h.times(1), 1), t, :].rearrange("p a c -> p (a c)"),
                                         start=(t == 0), stop=(t == s))
                last.then_inc(pv_done, 1)

            def stack_transposes(h):
                wait(pe, stack_ready, h.times(1, 0))
                for a, stack in enumerate((qst, kst)):
                    for s in range(SEQ_TILES):
                        last = pe.transpose(bank16(0)[0:STACK, SEQ * a + P * s:SEQ * a + P * s + P],
                                            stack[:, bass.ds(h.times(1), 1), s, :].rearrange("p a c -> p (a c)"),
                                            ident16[:, :])
                last.then_inc(stack_T, 1)

            def negmax_transposes(h):
                pe.wait_ge(negmax_ready, h.times(1, 1))
                wait(pe, negmax_stacked, h.times(1, 0))
                for s in range(SEQ_TILES):
                    last = pe.transpose(bank16(0)[STACK:P, P * s:P * s + P], negmax[:, h.parity, s, :],
                                        ident16[:, :])
                last.then_inc(negmax_T, 1)

            pe.wait_ge(projected, 4)
            pe.wait_ge(key_rows, 2)
            pipelined(pe, UNITS, 2, [(1, scores), (2, shifted), (3, weighted), (0, stack_transposes),
                                     (1, negmax_transposes)])
            pe.wait_ge(pv_done, UNITS)
            pe.sem_inc(attended, 1)

            def project(t):
                pe.wait_ge(o_T_ready, t.times(1, 1))
                wait(pe, o_y_stats, t.times(1, -1))
                for g in range(GROUPS):
                    last = pe.matmul(bank(1 + t.parity), o_T[:, t.parity, g, :], WoT[:, g, :],
                                     start=(g == 0), stop=(g == GROUPS - 1))
                last.then_inc(o_proj_done, 1)

            def o_transposes(t):
                pe.wait_ge(o_staged, t.times(1, 1))
                wait(pe, o_T_ready, t.times(1, 0))
                for g in range(GROUPS):
                    last = pe.transpose(PS[:, 0, P * g:P * g + P], o_in[:, t.parity, P * g:P * g + P],
                                        ident[:, :])
                last.then_inc(o_T_done, 1)

            def x2_transposes(t):
                pe.wait_ge(o_lo_ready, t.times(1, 1))
                wait(pe, o_x2T_ready, t.times(1, 0))
                for part in range(2):
                    for k in range(GROUPS):
                        at = P * (part * GROUPS + k)
                        last = pe.transpose(bank16(3)[:, at:at + P], o_parts[:, t.parity, part, P * k:P * k + P],
                                            ident16[:, :])
                last.then_inc(o_x2T_done, 1)

            pe.wait_ge(attended, 3)
            pipelined(pe, TILES, 4, [(1, project), (0, o_transposes), (3, x2_transposes)])
            pe.wait_ge(o_x2T_done, TILES)
            pe.sem_inc(mixed, 1)

            pe.wait_ge(mixed, 4)
            pe.wait_ge(wffn_in, 48)
            pe.sem_inc(down_done, 1)
            with pe.Fori(0, BATCH) as c:
                with pe.Fori(0, ITILES // 2) as j:
                    for u in range(2):
                        i = j * 2 + u
                        n = c * ITILES + i
                        for m, free, done in ((0, silu_ready, gate_done), (1, fuse_ready, up_done)):
                            pe.wait_ge(free, n + 1)
                            for k in range(GROUPS):
                                for part in range(2):
                                    last = pe.matmul(
                                        bank(2 * m + u), w_gu[:, m, k, bass.ds(i * P, P)],
                                        x2T[:, part * GROUPS + k, bass.ds(c * CHUNK, CHUNK)],
                                        start=(k == 0 and part == 0), stop=(k == GROUPS - 1 and part == 1))
                            last.then_inc(done, 1)
                for u in range(CTILES):
                    t = c * CTILES + u
                    pe.wait_ge(y_read, t + 1)
                    for i in range(ITILES):
                        if u == 0 and i in (0, ITILES - 2, ITILES - 1):
                            pe.wait_ge(flo_ready, c * ITILES + (max(i + 1, ITILES - 2) + PRIMED))
                        for part in range(2):
                            last = pe.matmul(bank(4 + u % 2), fused[:, part, i, P * u:P * u + P], w_dn[:, i, :],
                                             start=(i == 0 and part == 0), stop=(i == ITILES - 1 and part == 1))
                    last.then_inc(down_done, 1)


_INS = ["L0_attn_x", "L0_attn_Wq", "L0_attn_Wdkv", "L0_attn_Wuk", "L0_attn_Wuv", "L0_attn_ln_g", "L0_attn_ln_b",
        "L0_attn_Wo_h", "L0_attn_Wo", "L0_attn_bo", "L0_ffn_w_gate", "L0_ffn_w_up", "L0_ffn_w_down",
        "L0_ffn_s_gate", "L0_ffn_s_up", "L0_ffn_s_down"]


def kernel(**inputs):
    import numpy as np
    import concourse.bacc as bacc
    from concourse.bass_utils import run_bass_kernel_spmd

    nc = bacc.Bacc("TRN2", target_bir_lowering=False, num_devices=1)
    arrays, args = {}, []
    for name in _INS:
        a = np.ascontiguousarray(inputs[name])
        if a.dtype.itemsize == 1:
            a = a.view(np.int32)
        arrays[f"in_{name}"] = a
        args.append(nc.dram_tensor(f"in_{name}", a.shape, mybir.dt.from_np(a.dtype), kind="ExternalInput").ap())
    args.append(nc.dram_tensor("out_x", (BATCH, SEQ, EMB), mybir.dt.float32, kind="ExternalOutput").ap())
    block_kernel(nc, *args)
    r = run_bass_kernel_spmd(nc, [arrays], core_ids=[0])
    return r.results[0]["out_x"]
```

```python
import math
from contextlib import ExitStack

import concourse.bass as bass
from concourse import mybir

P = 128
BATCH, SEQ, EMB = 4, 512, 512
HEADS, HD, LAT = 16, 32, 128
INTER = 2048
TOKENS = BATCH * SEQ
TILES = TOKENS // P
SEQ_TILES = SEQ // P
UNITS = BATCH * HEADS
GROUPS = EMB // P
GH = P // HD
ITILES = INTER // P
CHUNK = 512
CTILES = CHUNK // P
STACK = 3 * HD
EPS = 1e-5
VH = HD + 1
VW = 2 * VH
X2_SCALE = 2048.0
KEY_BOUND = 256.0
VALUE_BOUND = 2048.0
LATENT_MAX = 11.5
FUSE_BOUND = 32000.0
RAW_BOUND = 2.0 ** 16
NEG = -1e30

SETUP_PE = ["mean", "wukT", "wuvT", "vecT", "bdqT", "bdoT", "A", "U", "G", "M", "N", "keybound", "keybias",
            "vb", "valuebound", "woT0", "woT1", "woT2", "woT3", "fuseT", "fuseall", "bo"]
SETUP_DVE = ["ones", "bdzero", "gmnzero", "Wc", "wukT", "vecT", "bdqT", "gA", "bA", "absA", "gU", "bU",
             "absU", "bounds", "G", "M", "N", "keybias", "vb", "fusemax", "fusered", "fusescale", "bo", "done"]
SETUP_ACT = ["wuvT", "bdoT", "woT0", "woT1", "woT2", "woT3"]


def nth(order, name):
    return order.index(name) + 1


class Step:

    def __init__(self, unit, loop, const):
        self.unit, self.loop, self.const = unit, loop, const

    def minus(self, lag):
        return Step(self.unit, self.loop, self.const - lag)

    def times(self, k, plus=0):
        whole = k * self.const + plus
        return whole if self.loop is None else self.loop * (k * self.unit) + whole

    @property
    def parity(self):
        return self.const % 2

    @property
    def slot(self):
        return self.const % 4

    @property
    def batch(self):
        q = self.const // self.unit
        return q if self.loop is None else self.loop + q

    @property
    def sub(self):
        return self.const % self.unit


def wait(eng, sem, value):
    if isinstance(value, int) and value <= 0:
        return
    eng.wait_ge(sem, value)


def wait_apart(eng, sem, value, tally):
    if isinstance(value, int) and value <= 0:
        return
    eng.wait_ge(sem, value)
    eng.sem_inc(tally, 1)


def pipelined(eng, n, unit, stages, peel=4):
    deepest = max(lag for lag, _ in stages)

    def step(s, base):
        for lag, fn in stages:
            at = s.minus(lag)
            if base is None or 0 <= base - lag < n:
                fn(at)

    for s in range(peel):
        step(Step(unit, None, s), s)
    with eng.Fori(peel // unit, n // unit) as loop:
        for u in range(unit):
            step(Step(unit, loop, u), None)
    for s in range(n, n + deepest):
        step(Step(unit, None, s), s)


def block_kernel(nc, x, Wq, Wdkv, Wuk, Wuv, ln_g, ln_b, Wo_h, Wo, bo, w_gate, w_up, w_down,
                 s_gate, s_up, s_down, out):
    f32, f16, bf16 = mybir.dt.float32, mybir.dt.float16, mybir.dt.bfloat16
    ALU, ACT, AX = mybir.AluOpType, mybir.ActivationFunctionType, mybir.AxisListType
    ctx = ExitStack()
    with ctx:
        def sb(name, shape, dt):
            return ctx.enter_context(nc.sbuf_tensor(name, shape, dt))

        def sem(name):
            return ctx.enter_context(nc.semaphore(name))

        ident = sb("ident", [P, P], f32)
        ident16 = sb("ident16", [P, P], f16)
        identb = sb("identb", [P, P], bf16)
        causalT = sb("causalT", [P, P], bf16)
        ones = sb("ones", [P, P], f32)
        headsum = sb("headsum", [P, GH], f32)
        halfneg = sb("halfneg", [P, 1], f32)
        vec = sb("vec", [P, 4 * HEADS], f32)
        sgate = sb("sgate", [P, ITILES], f32)
        sup = sb("sup", [P, ITILES], f32)
        kscale = sb("kscale", [P, 5], f32)
        small = sb("small", [P, 4, 96], f32)
        negmax = sb("negmax", [P, 2, SEQ_TILES, HD], f16)
        rowmax = sb("rowmax", [P, 2, SEQ_TILES], f32)
        rsum = sb("rsum", [P, SEQ_TILES], f32)
        scratch = sb("scratch", [P, 64], f32)
        GMN = sb("GMN", [P, GROUPS, 3, P], f32)
        keybias = sb("keybias", [P, EMB], f32)
        WoT = sb("WoT", [P, GROUPS, EMB], f32)
        bo_all = sb("bo_all", [P, EMB], f32)
        sdown = sb("sdown", [P, EMB], f32)
        TMP = sb("TMP", [P, 10 * EMB], f32)
        Q = sb("Q", [P, UNITS * SEQ_TILES * STACK], f16)
        K = sb("K", [P, UNITS * SEQ_TILES * STACK], f16)
        V = sb("V", [P, UNITS * SEQ_TILES * VW], f16)
        O = sb("O", [P, UNITS * SEQ_TILES * HD], f32)
        qst = Q[:, :].rearrange("p (n s c) -> p n s c", s=SEQ_TILES, c=STACK)
        kst = K[:, :].rearrange("p (n s c) -> p n s c", s=SEQ_TILES, c=STACK)
        vst = V[:, :].rearrange("p (n s c) -> p n s c", s=SEQ_TILES, c=VW)
        ost = O[:, :].rearrange("p (n s c) -> p n s c", s=SEQ_TILES, c=HD)

        def carve(t, start, shape, dt=f32):
            n = math.prod(shape)
            words = n if dt == f32 else n // 2
            v = t[:, start:start + words] if t.dtype == f32 else t[:, 2 * start:2 * (start + words)].bitcast(f32)
            v = v if dt == f32 else v.bitcast(dt)
            names = "abcd"[:len(shape)]
            return v.rearrange(f"p ({' '.join(names)}) -> p {' '.join(names)}",
                               **{k: s for k, s in zip(names[1:], shape[1:])}) if len(shape) > 1 else v

        wdkv_sb = carve(O, 0, [EMB])
        wuk_sb = carve(O, 512, [EMB])
        wuv_sb = carve(O, 1024, [EMB])
        bdq = carve(O, 1536, [GROUPS, P])
        bdo = carve(O, 2048, [GROUPS, P])
        wo_nat = carve(O, 2560, [GROUPS, EMB])
        bdqT = carve(O, 4608, [GROUPS, P])
        bdoT = carve(O, 5120, [GROUPS, P])
        wukT = carve(O, 5632, [GROUPS, P])
        wuvT = carve(O, 6144, [GROUPS, P])
        wc = carve(O, 6656, [EMB])
        vb_sb = carve(O, 7168, [GROUPS, P])
        vec_rows = carve(O, 7680, [P])
        gA, bA, absA, gU, bU, absU = (carve(V, EMB * n, [EMB]) for n in range(6))
        p_x = carve(TMP, 0, [4, EMB])
        p_ln = carve(TMP, 2048, [4, EMB])
        p_xT = carve(TMP, 4096, [2, GROUPS, P])
        p_prod = carve(O, 0, [2, GROUPS, P])
        p_key = carve(O, 1024, [4, EMB])
        p_value = carve(O, 3072, [4, EMB])
        gmn_flat = GMN[:, :, :, :].rearrange("p g m c -> p (g m c)")
        prob = carve(TMP, 0, [2, 1280])
        prob_parts = carve(TMP, 2560, [2, 2, 1280], f16)
        qk = gmn_flat[:, 0:1024].bitcast(f16).rearrange("p (b a t) -> p b a t", b=2, a=2)
        causal = gmn_flat[:, 1024:1024 + SEQ]
        o_x = carve(TMP, 0, [2, EMB])
        o_in = carve(TMP, 1024, [2, EMB])
        o_T = carve(TMP, 2048, [2, GROUPS, P])
        o_y = carve(TMP, 3072, [2, EMB])
        o_x2 = gmn_flat[:, 0:EMB]
        o_parts = gmn_flat[:, EMB:3 * EMB].bitcast(f16).rearrange("p (b h c) -> p b h c", b=2, h=2)
        w_gu = V[:, 0:2 * GROUPS * INTER].rearrange("p (m k n) -> p m k n", m=2, k=GROUPS)
        x2T = K[:, 0:2 * GROUPS * TOKENS].rearrange("p (h k t) -> p (h k) t", h=2, k=GROUPS)
        fused = Q[:, 0:2 * ITILES * CHUNK].rearrange("p (h i t) -> p h i t", h=2, i=ITILES)
        w_dn = Q[:, 2 * ITILES * CHUNK:3 * ITILES * CHUNK].rearrange("p (i n) -> p i n", i=ITILES)
        f_silu = carve(TMP, 0, [2, CHUNK])
        f_prod = carve(TMP, 1024, [2, CHUNK])
        f_y = carve(TMP, 2048, [2, EMB])
        f_out = WoT[:, :, :]

        SCORE_AT = [(2, 384), (3, 0), (2, 0), (1, 0)]
        SHIFTED_AT = [(4, 0), (5, 0), (6, 0), (5, 384)]
        PROB_AT = [0, 512, 1024, 896]

        PS = ctx.enter_context(nc.psum_tensor("PS", [P, 8, 512], f32))

        def bank(n):
            return PS[:, n, :]

        def bank16(n):
            return PS[:, n, :].bitcast(f16)

        pv = PS[:, 7, 0:SEQ_TILES * VH].rearrange("p (s c) -> p s c", c=VH)

        def by_head(ap):
            return ap.rearrange("p (h c) -> p h c", c=HD)

        tally = sem("tally")
        consts_ready = sem("consts_ready")
        wdkv_in = sem("wdkv_in")
        heads_in = sem("heads_in")
        vecs_in = sem("vecs_in")
        blockdiag_in = sem("blockdiag_in")
        wo_in = sem("wo_in")
        rows_in = sem("rows_in")
        setup_pe = sem("setup_pe")
        setup_dve = sem("setup_dve")
        setup_act = sem("setup_act")
        setup_chain = sem("setup_chain")
        p_x_in = [sem(f"p_x_in{n}") for n in range(4)]
        p_stats_chain = sem("p_stats_chain")
        p_stats = sem("p_stats")
        p_rstd = sem("p_rstd")
        p_shift = sem("p_shift")
        p_ln_ready = sem("p_ln_ready")
        p_hi_ready = sem("p_hi_ready")
        p_lo_ready = sem("p_lo_ready")
        p_T_done = sem("p_T_done")
        p_xT_ready = sem("p_xT_ready")
        p_G_done = sem("p_G_done")
        p_MN_done = sem("p_MN_done")
        p_prod_ready = sem("p_prod_ready")
        p_var_done = sem("p_var_done")
        p_var_eps = sem("p_var_eps")
        p_root_ready = sem("p_root_ready")
        p_newton_chain = sem("p_newton_chain")
        p_key_raw = sem("p_key_raw")
        p_key_ready = sem("p_key_ready")
        p_khi_ready = sem("p_khi_ready")
        p_klo_ready = sem("p_klo_ready")
        p_value_ready = sem("p_value_ready")
        p_vhi_ready = sem("p_vhi_ready")
        p_vlo_ready = sem("p_vlo_ready")
        projected = sem("projected")
        att_consts = sem("att_consts")
        key_rows = sem("key_rows")
        att_mask = sem("att_mask")
        stack_T = sem("stack_T")
        stack_ready = sem("stack_ready")
        scores_done = sem("scores_done")
        max_done = sem("max_done")
        negmax_chain = sem("negmax_chain")
        negmax_ready = sem("negmax_ready")
        negmax_T = sem("negmax_T")
        negmax_stacked = sem("negmax_stacked")
        shifted_done = sem("shifted_done")
        prob_ready = sem("prob_ready")
        prob_hi_ready = sem("prob_hi_ready")
        prob_lo_ready = sem("prob_lo_ready")
        pv_done = sem("pv_done")
        rsum_ready = sem("rsum_ready")
        o_stored = sem("o_stored")
        attended = sem("attended")
        o_x_in = [sem(f"o_x_in{n}") for n in range(4)]
        o_staged = sem("o_staged")
        o_T_done = sem("o_T_done")
        o_T_ready = sem("o_T_ready")
        o_proj_done = sem("o_proj_done")
        o_y_chain = sem("o_y_chain")
        o_y_stats = sem("o_y_stats")
        o_y_pool = sem("o_y_pool")
        o_y_rstd = sem("o_y_rstd")
        o_y_ln = sem("o_y_ln")
        o_x1_chain = sem("o_x1_chain")
        o_x1_stats = sem("o_x1_stats")
        o_x1_pool = sem("o_x1_pool")
        o_x1_rstd = sem("o_x1_rstd")
        o_x2_ready = sem("o_x2_ready")
        o_hi_ready = sem("o_hi_ready")
        o_lo_ready = sem("o_lo_ready")
        o_x2T_done = sem("o_x2T_done")
        o_x2T_ready = sem("o_x2T_ready")
        wffn_in = sem("wffn_in")
        mixed = sem("mixed")
        gate_done = sem("gate_done")
        up_done = sem("up_done")
        silu_ready = sem("silu_ready")
        fuse_ready = sem("fuse_ready")
        fhi_ready = sem("fhi_ready")
        flo_ready = sem("flo_ready")
        down_done = sem("down_done")
        y_read = sem("y_read")
        y_chain = sem("y_chain")
        y_stats = sem("y_stats")
        y_pool = sem("y_pool")
        y_rstd = sem("y_rstd")
        y_ln = sem("y_ln")
        out_ready = sem("out_ready")
        chunk_stored = sem("chunk_stored")
        out_stored = sem("out_stored")
        PRIMED = 2

        w_gate, w_up, w_down = (w.bitcast(mybir.dt.int8) for w in (w_gate, w_up, w_down))
        x_tiles = x.rearrange("b (s p) e -> p (b s) e", p=P)
        out_tiles = out.rearrange("b (s p) e -> p (b s) e", p=P)

        def heads_of(t, stack, lo, hi):
            return stack[:, bass.ds(t.batch * HEADS, HEADS), t.sub, lo:hi]

        def arrived(eng, sems, t):
            eng.wait_ge(sems[t.slot], (t.batch + 1) * 16)

        def across(r):
            return r.unsqueeze(2).to_broadcast([P, HEADS, HD])

        block = ctx.enter_context(nc.Block())

        @block.sync
        def _(sp):
            sp.dma_start(by_head(wdkv_sb), Wdkv.rearrange("h l d -> l h d")).then_inc(wdkv_in, 16)
            sp.dma_start(by_head(wuk_sb), Wuk.rearrange("h l d -> l h d")).then_inc(heads_in, 16)
            sp.dma_start(by_head(wuv_sb), Wuv.rearrange("h l d -> l h d")).then_inc(heads_in, 16)
            for n, v in enumerate((ln_g, ln_b, s_gate.rearrange("(c p) -> c p", p=P),
                                   s_up.rearrange("(c p) -> c p", p=P))):
                sp.dma_start(vec_rows[16 * n:16 * n + 16, :], v).then_inc(vecs_in, 16)
            sp.wait_ge(setup_dve, nth(SETUP_DVE, "bdzero"))
            for a in range(GH):
                for dst, w in ((bdq, Wq), (bdo, Wo_h)):
                    sp.dma_start(dst[HD * a:HD * a + HD, :, HD * a:HD * a + HD],
                                 w.rearrange("(g a) i j -> a i g j", a=GH)[a]).then_inc(blockdiag_in, 16)
            sp.dma_start(wo_nat, Wo.rearrange("(m p) n -> p m n", p=P)).then_inc(wo_in, 16)
            sp.dma_start(bo_all[:, :], bo.partition_broadcast(P)).then_inc(rows_in, 16)
            sp.dma_start(sdown[:, :], s_down.partition_broadcast(P)).then_inc(rows_in, 16)

            def load_x(dst, buffer, sems, t):
                sp.dma_start(dst[:, buffer, :], x_tiles[:, bass.ds(t.times(1), 1), :]
                             .rearrange("p a e -> p (a e)")).then_inc(sems[t.slot], 16)

            def load_p_x(t):
                wait(sp, p_ln_ready, t.times(1, -3))
                load_x(p_x, t.slot, p_x_in, t)

            def load_o_x(t):
                wait(sp, o_x1_stats, t.times(1, -1))
                load_x(o_x, t.parity, o_x_in, t)

            pipelined(sp, TILES, 4, [(0, load_p_x)])
            sp.wait_ge(attended, 4)
            pipelined(sp, TILES, 4, [(0, load_o_x)])
            sp.sem_inc(chunk_stored, 1)
            with sp.Fori(0, BATCH) as c:
                for u in range(CTILES):
                    sp.wait_ge(out_ready, c * CTILES + (u + 2))
                    sp.dma_start(out_tiles[:, bass.ds(c * CTILES + u, 1), :].rearrange("p a e -> p (a e)"),
                                 f_out[:, u, :]).then_inc(out_stored, 16)
                sp.wait_ge(out_stored, (c + 1) * (16 * CTILES))
                sp.sem_inc(chunk_stored, 1)
            sp.wait_ge(out_stored, 16 * TILES)

        @block.gpsimd
        def _(pool):
            for m, v in ((ident, 0.0), (ident16, 0.0), (identb, 0.0), (causalT, 0.0), (halfneg, -0.5)):
                pool.memset(m[:, :], v).then_inc(consts_ready, 1)
            pool.wait_ge(consts_ready, 5)
            for m in (ident, ident16, identb):
                pool.affine_select(out=m[:, :], in_=m[:, :], compare_op=ALU.not_equal, fill=1.0, base=0,
                                   pattern=[[-1, P]], channel_multiplier=1).then_inc(consts_ready, 1)
            pool.affine_select(out=causalT[:, :], in_=causalT[:, :], compare_op=ALU.is_ge, fill=NEG, base=0,
                               pattern=[[1, P]], channel_multiplier=-1).then_inc(consts_ready, 1)

            def rstd(st, stats, used, chain, done, t, gain=None):
                links = 2 if gain is None else 3
                pool.wait_ge(stats, t.times(1, 1))
                wait_apart(pool, used, t.times(1, -1), tally)
                pool.tensor_scalar(st[:, 8:9], st[:, 7:8], EPS, None, ALU.add).then_inc(chain, 1)
                pool.wait_ge(chain, t.times(links, 1))
                pool.tensor_tensor(st[:, 9:10], st[:, 8:9], halfneg[:, :], ALU.pow).then_inc(chain, 1)
                wait_apart(pool, chain, t.times(links, 2), tally)
                if gain is not None:
                    pool.tensor_scalar(st[:, 9:10], st[:, 9:10], gain, None, ALU.mult).then_inc(chain, 1)
                    wait_apart(pool, chain, t.times(links, 3), tally)
                pool.tensor_scalar(st[:, 10:11], st[:, 6:7], st[:, 9:10], -1.0, ALU.mult, ALU.mult)\
                    .then_inc(done, 1)

            def x_scale(t):
                st = small[:, t.slot, :]
                pool.wait_ge(p_stats, t.times(1, 1))
                pool.tensor_tensor(st[:, 9:10], st[:, 8:9], halfneg[:, :], ALU.pow).then_inc(p_rstd, 1)

            def x_low(t):
                pool.wait_ge(p_hi_ready, t.times(1, 1))
                pool.tensor_tensor(heads_of(t, qst, HD, 2 * HD), by_head(p_ln[:, t.slot, :]),
                                   heads_of(t, qst, 0, HD), ALU.subtract).then_inc(p_lo_ready, 1)

            def key_bias(t):
                pool.wait_ge(p_key_raw, t.times(1, 1))
                pool.tensor_tensor(p_key[:, t.slot, :], p_key[:, t.slot, :], keybias[:, :], ALU.add)\
                    .then_inc(p_key_ready, 1)

            def value_low(t):
                pool.wait_ge(p_vhi_ready, t.times(1, 1))
                pool.tensor_tensor(heads_of(t, vst, VH, VH + HD), by_head(p_value[:, t.slot, :]),
                                   heads_of(t, vst, 0, HD), ALU.subtract).then_inc(p_vlo_ready, 1)

            pool.wait_ge(consts_ready, 9)
            pipelined(pool, TILES, 4, [(2, x_low), (0, x_scale), (4, key_bias), (5, value_low)], peel=8)
            pool.wait_ge(p_vlo_ready, TILES)
            pool.sem_inc(projected, 1)

            pool.wait_ge(projected, 4)
            pool.memset(causal, 0.0).then_inc(att_consts, 1)
            pool.wait_ge(att_consts, 1)
            pool.affine_select(out=causal[:, SEQ - P:], in_=causal[:, SEQ - P:], compare_op=ALU.is_ge, fill=NEG,
                               base=0, pattern=[[-1, P]], channel_multiplier=1).then_inc(att_mask, 1)

            def prob_low(h):
                pool.wait_ge(prob_hi_ready, h.times(1, 1))
                pool.tensor_tensor(prob_parts[:, h.parity, 1, :], prob[:, h.parity, :],
                                   prob_parts[:, h.parity, 0, :], ALU.subtract).then_inc(prob_lo_ready, 1)

            pipelined(pool, UNITS, 2, [(0, prob_low)], peel=6)
            pool.wait_ge(prob_lo_ready, UNITS)
            pool.sem_inc(attended, 1)

            pool.wait_ge(attended, 4)
            for m, w in enumerate((w_gate, w_up)):
                pool.dma_start(w_gu[:, m, :, :], w.rearrange("(k p) n -> p k n", p=P)).then_inc(wffn_in, 16)
            pool.dma_start(w_dn, w_down.rearrange("(i p) n -> p i n", p=P)).then_inc(wffn_in, 16)

            def y_scale(t):
                rstd(small[:, t.parity, :], o_y_stats, o_y_ln, o_y_pool, o_y_rstd, t)

            def x1_scale(t):
                rstd(small[:, t.parity, 32:], o_x1_stats, o_x2_ready, o_x1_pool, o_x1_rstd, t, gain=X2_SCALE)

            def x2_low(t):
                pool.wait_ge(o_hi_ready, t.times(1, 1))
                pool.tensor_tensor(o_parts[:, t.parity, 1, :], o_x2, o_parts[:, t.parity, 0, :], ALU.subtract)\
                    .then_inc(o_lo_ready, 1)

            pipelined(pool, TILES, 4, [(2, x1_scale), (1, y_scale), (2, x2_low)])
            pool.wait_ge(o_lo_ready, TILES)
            pool.sem_inc(mixed, 1)

            pool.wait_ge(mixed, 4)
            pool.sem_inc(flo_ready, PRIMED)
            with pool.Fori(0, BATCH) as c:
                with pool.Fori(0, ITILES // 2) as j:
                    for u in range(2):
                        i = j * 2 + u
                        pool.wait_ge(fhi_ready, c * ITILES + i + (1 + PRIMED))
                        pool.tensor_tensor(fused[:, 1, bass.ds(i, 1), :].rearrange("p a t -> p (a t)"),
                                           f_prod[:, u, :],
                                           fused[:, 0, bass.ds(i, 1), :].rearrange("p a t -> p (a t)"),
                                           ALU.subtract).then_inc(flo_ready, 1)
                for u in range(CTILES):
                    t = c * CTILES + u
                    st = small[:, u % 2, :]
                    wait_apart(pool, y_stats, t + 1, tally)
                    pool.tensor_scalar(st[:, 8:9], st[:, 7:8], EPS, None, ALU.add).then_inc(y_pool, 1)
                    pool.wait_ge(y_pool, t * 2 + 1)
                    pool.wait_ge(y_ln, t + 1)
                    pool.tensor_tensor(st[:, 9:10], st[:, 8:9], halfneg[:, :], ALU.pow).then_inc(y_pool, 1)
                    wait_apart(pool, y_pool, t * 2 + 2, tally)
                    pool.tensor_scalar(st[:, 10:11], st[:, 6:7], st[:, 9:10], -1.0, ALU.mult, ALU.mult)\
                        .then_inc(y_rstd, 1)

        @block.scalar
        def _(act):
            for name, n, dst in (("wuvT", 2, wuvT), ("bdoT", 4, bdoT)):
                act.wait_ge(setup_pe, nth(SETUP_PE, name))
                act.activation(dst.rearrange("p g c -> p (g c)"), bank(n), ACT.Copy).then_inc(setup_act, 1)
            act.wait_ge(setup_dve, nth(SETUP_DVE, "bounds"))
            for k in range(GROUPS):
                act.wait_ge(setup_pe, nth(SETUP_PE, f"woT{k}"))
                act.activation(WoT[:, k, :], bank(6 + k % 2), ACT.Copy, scale=kscale[:, 3:4]).then_inc(setup_act, 1)

            def ln(t):
                st = small[:, t.slot, :]
                act.wait_ge(p_shift, t.times(1, 1))
                wait(act, p_lo_ready, t.times(1, -3))
                wait(act, p_T_done, t.times(1, -3))
                act.activation(p_ln[:, t.slot, :], p_x[:, t.slot, :], ACT.Identity,
                               scale=st[:, 9:10], bias=st[:, 10:11]).then_inc(p_ln_ready, 1)

            def x_high(t):
                act.wait_ge(p_ln_ready, t.times(1, 1))
                act.activation(heads_of(t, qst, 0, HD), by_head(p_ln[:, t.slot, :]), ACT.Copy)\
                    .then_inc(p_hi_ready, 1)

            def xT(t):
                act.wait_ge(p_T_done, t.times(1, 1))
                wait(act, p_prod_ready, t.times(1, -1))
                wait(act, p_MN_done, t.times(1, -1))
                act.activation(p_xT[:, t.parity, :, :].rearrange("p g c -> p (g c)"), bank(0), ACT.Copy)\
                    .then_inc(p_xT_ready, 1)

            def root(t):
                st = small[:, t.slot, 16:]
                act.wait_ge(p_var_eps, t.times(1, 1))
                act.activation(st[:, 16:32], st[:, 0:16], ACT.Sqrt).then_inc(p_root_ready, 1)

            def key_high(t):
                act.wait_ge(p_key_ready, t.times(1, 1))
                act.activation(heads_of(t, kst, 0, HD), by_head(p_key[:, t.slot, :]), ACT.Copy)\
                    .then_inc(p_khi_ready, 1)

            def value_high(t):
                act.wait_ge(p_value_ready, t.times(1, 1))
                act.activation(heads_of(t, vst, 0, HD), by_head(p_value[:, t.slot, :]), ACT.Copy)\
                    .then_inc(p_vhi_ready, 1)

            pipelined(act, TILES, 4, [(1, ln), (3, root), (1, x_high), (1, xT), (4, key_high), (4, value_high)], peel=8)
            act.wait_ge(p_khi_ready, TILES)
            act.wait_ge(p_vhi_ready, TILES)
            act.wait_ge(p_xT_ready, TILES)
            act.sem_inc(projected, 1)

            def exps(h):
                act.wait_ge(shifted_done, h.times(1, 1))
                wait(act, prob_lo_ready, h.times(1, -1))
                act.activation(prob[:, h.parity, 0:1024], PS[:, 4:6, :].rearrange("p a t -> p (a t)"), ACT.Exp,
                               scale=kscale[:, 2:3])
                act.activation(prob[:, h.parity, 1024:1280], PS[:, 6, 0:256], ACT.Exp,
                               scale=kscale[:, 2:3]).then_inc(prob_ready, 1)
                act.wait_ge(prob_ready, h.times(1, 1))
                wait(act, pv_done, h.times(1, -1))
                act.activation(prob_parts[:, h.parity, 0, :], prob[:, h.parity, :], ACT.Copy)\
                    .then_inc(prob_hi_ready, 1)

            act.wait_ge(projected, 4)
            pipelined(act, UNITS, 2, [(0, exps)], peel=6)
            act.wait_ge(prob_hi_ready, UNITS)
            act.sem_inc(attended, 1)

            def stage_o(t):
                wait(act, o_T_done, t.times(1, -1))
                act.activation(by_head(o_in[:, t.parity, :]), heads_of(t, ost, 0, HD), ACT.Copy)\
                    .then_inc(o_staged, 1)

            def oT(t):
                act.wait_ge(o_T_done, t.times(1, 1))
                wait(act, o_proj_done, t.times(1, -1))
                act.activation(o_T[:, t.parity, :, :].rearrange("p g c -> p (g c)"), bank(0), ACT.Copy)\
                    .then_inc(o_T_ready, 1)

            def y_norm(t):
                st = small[:, t.parity, :]
                act.wait_ge(o_y_rstd, t.times(1, 1))
                act.activation(o_y[:, t.parity, :], o_y[:, t.parity, :], ACT.Identity,
                               scale=st[:, 9:10], bias=st[:, 10:11]).then_inc(o_y_ln, 1)

            def x2_high(t):
                act.wait_ge(o_x2_ready, t.times(1, 1))
                wait(act, o_x2T_done, t.times(1, -1))
                act.activation(o_parts[:, t.parity, 0, :], o_x2, ACT.Copy).then_inc(o_hi_ready, 1)

            def x2_T(t):
                act.wait_ge(o_x2T_done, t.times(1, 1))
                act.activation(x2T[:, :, bass.ds(t.times(P), P)],
                               bank16(3).rearrange("p (k c) -> p k c", c=P), ACT.Copy).then_inc(o_x2T_ready, 1)

            act.wait_ge(attended, 4)
            pipelined(act, TILES, 4, [(0, stage_o), (0, oT), (1, y_norm), (2, x2_high), (3, x2_T)])
            act.wait_ge(o_x2T_ready, TILES)
            act.sem_inc(mixed, 1)

            act.wait_ge(mixed, 4)
            for primed in (silu_ready, fhi_ready, y_ln):
                act.sem_inc(primed, PRIMED)
            with act.Fori(0, BATCH) as c:
                act.wait_ge(down_done, c * CTILES + 1)
                with act.Fori(0, ITILES // 2) as j:
                    for u in range(2):
                        i = j * 2 + u
                        act.wait_ge(gate_done, c * ITILES + i + 1)
                        act.wait_ge(fuse_ready, c * ITILES + i + 1)
                        act.activation(f_silu[:, u, :], bank(u), ACT.Silu, scale=sgate[:, bass.ds(i, 1)])\
                            .then_inc(silu_ready, 1)
                        act.wait_ge(fuse_ready, c * ITILES + i + (1 + PRIMED))
                        act.activation(fused[:, 0, bass.ds(i, 1), :].rearrange("p a t -> p (a t)"),
                                       f_prod[:, u, :], ACT.Copy).then_inc(fhi_ready, 1)
                for u in range(CTILES):
                    st = small[:, u % 2, :]
                    act.wait_ge(y_rstd, c * CTILES + (u + 1))
                    act.activation(f_y[:, u % 2, :], f_y[:, u % 2, :], ACT.Identity,
                                   scale=st[:, 9:10], bias=st[:, 10:11]).then_inc(y_ln, 1)

        @block.vector
        def _(dve):
            links = [0]

            def link(ins):
                links[0] += 1
                ins.then_inc(setup_chain, 1)
                dve.wait_ge(setup_chain, links[0])

            def absolute(out, a):
                return dve.scalar_tensor_tensor(out, a, -1.0, a, ALU.mult, ALU.max)

            dve.memset(ones[:, :], 1.0).then_inc(setup_dve, 1)
            dve.memset(bdq, 0.0)
            dve.memset(bdo, 0.0).then_inc(setup_dve, 1)
            dve.memset(GMN[:, :, :, :], 0.0).then_inc(setup_dve, 1)
            dve.memset(negmax[:, :, :, :], 0.0)
            link(dve.memset(headsum[:, :], 0.0))
            for a in range(GH):
                dve.memset(headsum[HD * a:HD * a + HD, a:a + 1], 1.0)

            dve.wait_ge(wdkv_in, 16)
            dve.wait_ge(setup_pe, nth(SETUP_PE, "mean"))
            dve.scalar_tensor_tensor(wc, bank(0), -1.0 / LAT, wdkv_sb, ALU.mult, ALU.add).then_inc(setup_dve, 1)
            for name, n, dst in (("wukT", 1, wukT.rearrange("p g c -> p (g c)")), ("vecT", 5, vec[:, :]),
                                 ("bdqT", 3, bdqT.rearrange("p g c -> p (g c)"))):
                dve.wait_ge(setup_pe, nth(SETUP_PE, name))
                dve.tensor_copy(dst, PS[:, n, 0:dst.shape[1]]).then_inc(setup_dve, 1)
            dve.wait_ge(setup_dve, nth(SETUP_DVE, "vecT"))
            g, b = vec[:, 0:HEADS], vec[:, HEADS:2 * HEADS]
            absolute(scratch[:, 0:16], g)
            link(absolute(scratch[:, 16:32], b))
            link(dve.scalar_tensor_tensor(scratch[:, 32:48], scratch[:, 0:16], LATENT_MAX, scratch[:, 16:32],
                                          ALU.mult, ALU.add))
            dve.wait_ge(setup_pe, nth(SETUP_PE, "A"))
            dve.tensor_tensor(by_head(gA), by_head(bank(6)), across(g), ALU.mult).then_inc(setup_dve, 1)
            dve.tensor_tensor(by_head(bA), by_head(bank(6)), across(b), ALU.mult).then_inc(setup_dve, 1)
            link(dve.tensor_tensor(by_head(absA), by_head(bank(6)), across(scratch[:, 32:48]), ALU.mult))
            absolute(absA, absA).then_inc(setup_dve, 1)
            dve.wait_ge(setup_pe, nth(SETUP_PE, "U"))
            dve.tensor_tensor(by_head(gU), by_head(bank(7)), across(g), ALU.mult).then_inc(setup_dve, 1)
            dve.tensor_tensor(by_head(bU), by_head(bank(7)), across(b), ALU.mult).then_inc(setup_dve, 1)
            link(dve.tensor_tensor(by_head(absU), by_head(bank(7)), across(scratch[:, 32:48]), ALU.mult))
            absolute(absU, absU).then_inc(setup_dve, 1)

            for n, name, at, most in ((6, "keybound", 0, KEY_BOUND), (7, "valuebound", 3, VALUE_BOUND)):
                dve.wait_ge(setup_pe, nth(SETUP_PE, name))
                link(dve.tensor_reduce(kscale[:, at:at + 1], bank(n), AX.X, ALU.max))
                link(dve.tensor_scalar(kscale[:, at:at + 1], kscale[:, at:at + 1], 1e-30, 1.0 / most,
                                       ALU.max, ALU.mult))
            link(dve.reciprocal(kscale[:, 1:2], kscale[:, 0:1]))
            link(dve.tensor_scalar(kscale[:, 2:3], kscale[:, 0:1], 1.0 / math.sqrt(LAT), None, ALU.mult))
            dve.reciprocal(kscale[:, 4:5], kscale[:, 3:4]).then_inc(setup_dve, 1)
            dve.wait_ge(setup_dve, nth(SETUP_DVE, "bounds"))
            for m, name in enumerate(("G", "M", "N")):
                dve.wait_ge(setup_pe, nth(SETUP_PE, name))
                for a in range(GH):
                    rows = slice(HD * a, HD * a + HD)
                    src = bank(m).rearrange("p (g c) -> p g c", c=P)[rows, :, rows]
                    last = dve.tensor_scalar(GMN[rows, :, m, rows], src,
                                             (1.0 / LAT, kscale[rows, 1:2], kscale[rows, 4:5])[m], None, ALU.mult)
                last.then_inc(setup_dve, 1)
            dve.wait_ge(setup_pe, nth(SETUP_PE, "keybias"))
            dve.tensor_scalar(keybias[:, :], bank(4), kscale[:, 1:2], None, ALU.mult).then_inc(setup_dve, 1)
            dve.wait_ge(setup_pe, nth(SETUP_PE, "vb"))
            dve.tensor_scalar(vb_sb.rearrange("p g c -> p (g c)"), bank(5), kscale[:, 4:5], None, ALU.mult)\
                .then_inc(setup_dve, 1)

            link(dve.tensor_tensor(scratch[:, 0:16], vec[:, 32:48], vec[:, 48:64], ALU.mult))
            link(absolute(scratch[:, 0:16], scratch[:, 0:16]))
            dve.tensor_reduce(scratch[:, 16:17], scratch[:, 0:16], AX.X, ALU.max).then_inc(setup_dve, 1)
            dve.wait_ge(setup_pe, nth(SETUP_PE, "fuseT"))
            dve.tensor_reduce(scratch[0:1, 17:18], bank(3)[0:1, 0:P], AX.X, ALU.max).then_inc(setup_dve, 1)
            dve.wait_ge(setup_pe, nth(SETUP_PE, "fuseall"))
            link(dve.tensor_scalar(scratch[:, 18:19], bank(3)[:, 0:1], 1e-30, RAW_BOUND ** 2 / FUSE_BOUND,
                                   ALU.max, ALU.mult))
            link(dve.reciprocal(scratch[:, 19:20], scratch[:, 18:19]))
            dve.tensor_scalar(sgate[:, :], vec[:, 32:48], 1.0 / X2_SCALE, None, ALU.mult)
            dve.tensor_scalar(sup[:, :], vec[:, 48:64], scratch[:, 19:20], 1.0 / X2_SCALE, ALU.mult, ALU.mult)
            dve.wait_ge(rows_in, 32)
            dve.tensor_scalar(sdown[:, :], sdown[:, :], scratch[:, 18:19], None, ALU.mult).then_inc(setup_dve, 1)
            dve.wait_ge(setup_pe, nth(SETUP_PE, "bo"))
            dve.tensor_tensor(bo_all[:, :], bank(5), bo_all[:, :], ALU.add).then_inc(setup_dve, 1)
            dve.memset(vst[:, :, :, HD:VH], 1.0)
            dve.memset(vst[:, :, :, VW - 1:VW], 0.0).then_inc(setup_dve, 1)

            def x_stats(t):
                st = small[:, t.slot, :]
                arrived(dve, p_x_in, t)
                wait(dve, p_ln_ready, t.times(1, -3))
                dve.bn_stats(st[:, 0:6], p_x[:, t.slot, :]).then_inc(p_stats_chain, 1)

            def x_aggregate(t):
                st = small[:, t.slot, :]
                wait_apart(dve, p_stats_chain, t.times(2, 1), tally)
                dve.bn_aggr(st[:, 6:8], st[:, 0:6]).then_inc(p_stats_chain, 1)

            def x_var_eps(t):
                st = small[:, t.slot, :]
                dve.wait_ge(p_stats_chain, t.times(2, 2))
                dve.tensor_scalar(st[:, 8:9], st[:, 7:8], EPS, None, ALU.add).then_inc(p_stats, 1)

            def x_shift(t):
                st = small[:, t.slot, :]
                dve.wait_ge(p_rstd, t.times(1, 1))
                dve.scalar_tensor_tensor(st[:, 10:11], st[:, 6:7], -1.0, st[:, 9:10], ALU.mult, ALU.mult)\
                    .then_inc(p_shift, 1)

            def product(t):
                dve.wait_ge(p_G_done, t.times(1, 1))
                wait(dve, p_var_done, t.times(1, -1))
                dve.tensor_tensor(p_prod[:, t.parity, :, :].rearrange("p g c -> p (g c)"), bank(1),
                                  p_xT[:, t.parity, :, :].rearrange("p g c -> p (g c)"), ALU.mult)\
                    .then_inc(p_prod_ready, 1)

            def newton(t):
                st = small[:, t.slot, 16:]
                return st[:, 0:16], st[:, 32:48], st[:, 48:64]

            def inverse(t):
                a, y, s = newton(t)
                dve.wait_ge(p_root_ready, t.times(1, 1))
                dve.reciprocal(y, small[:, t.slot, 32:48]).then_inc(p_newton_chain, 1)

            def squared(t):
                a, y, s = newton(t)
                dve.wait_ge(p_newton_chain, t.times(5, 1))
                dve.tensor_tensor(s, y, y, ALU.mult).then_inc(p_newton_chain, 1)

            def by_variance(t):
                a, y, s = newton(t)
                dve.wait_ge(p_newton_chain, t.times(5, 2))
                dve.tensor_tensor(s, s, a, ALU.mult).then_inc(p_newton_chain, 1)

            def correction(t):
                a, y, s = newton(t)
                dve.wait_ge(p_newton_chain, t.times(5, 3))
                dve.tensor_scalar(s, s, -0.5, 1.5, ALU.mult, ALU.add).then_inc(p_newton_chain, 1)

            def refined(t):
                a, y, s = newton(t)
                dve.wait_ge(p_newton_chain, t.times(5, 4))
                dve.tensor_tensor(y, y, s, ALU.mult).then_inc(p_newton_chain, 1)

            def key_raw(t):
                dve.wait_ge(p_newton_chain, t.times(5, 5))
                dve.wait_ge(p_MN_done, t.times(1, 1))
                wait(dve, p_klo_ready, t.times(1, -3))
                dve.tensor_tensor(by_head(p_key[:, t.slot, :]), by_head(bank(4 + t.parity)),
                                  across(small[:, t.slot, 48:64]), ALU.mult).then_inc(p_key_raw, 1)

            def var_eps(t):
                dve.wait_ge(p_var_done, t.times(1, 1))
                dve.tensor_scalar(small[:, t.slot, 16:32], bank(3)[:, 0:HEADS], 0.0, EPS, ALU.max, ALU.add)\
                    .then_inc(p_var_eps, 1)

            def value(t):
                wait(dve, p_vlo_ready, t.times(1, -3))
                dve.tensor_tensor(by_head(p_value[:, t.slot, :]), by_head(bank(6 + t.parity)),
                                  across(small[:, t.slot, 48:64]), ALU.mult).then_inc(p_value_ready, 1)

            def x_high_again(t):
                dve.wait_ge(p_hi_ready, t.times(1, 1))
                dve.tensor_copy(heads_of(t, qst, 2 * HD, STACK), heads_of(t, qst, 0, HD))

            def key_high_again(t):
                dve.wait_ge(p_khi_ready, t.times(1, 1))
                dve.tensor_copy(heads_of(t, kst, HD, 2 * HD), heads_of(t, kst, 0, HD))

            def key_low(t):
                dve.wait_ge(p_khi_ready, t.times(1, 1))
                dve.tensor_tensor(heads_of(t, kst, 2 * HD, STACK), by_head(p_key[:, t.slot, :]),
                                  heads_of(t, kst, 0, HD), ALU.subtract).then_inc(p_klo_ready, 1)

            pipelined(dve, TILES, 4, [(1, x_shift), (0, x_stats), (2, product), (3, inverse), (0, x_aggregate), (2, x_high_again), (3, squared), (0, x_var_eps), (5, key_high_again), (3, by_variance), (5, key_low), (3, correction), (2, var_eps), (3, refined), (3, key_raw), (3, value)], peel=8)
            dve.wait_ge(p_klo_ready, TILES)
            dve.sem_inc(projected, 1)

            dve.wait_ge(projected, 4)
            dve.memset(qk[STACK:P, :, 1, :], 0.0).then_inc(key_rows, 1)
            dve.wait_ge(key_rows, 1)
            dve.memset(qk[STACK:STACK + 2, :, 1, :], 1.0).then_inc(key_rows, 1)
            dve.wait_ge(att_mask, 1)

            def maxima(h):
                wait_apart(dve, scores_done, h.times(1, 1), tally)
                for s, (n, at) in enumerate(SCORE_AT):
                    width = (s + 1) * P
                    last = dve.tensor_tensor_reduce(
                        out=PS[:, n, at:at + width], in0=PS[:, n, at:at + width], in1=causal[:, SEQ - width:],
                        scale=1.0, scalar=NEG, op0=ALU.add, op1=ALU.max,
                        accum_out=rowmax[:, h.parity, s:s + 1])
                last.then_inc(max_done, 1)

            def negmax_high(h):
                dve.wait_ge(max_done, h.times(1, 1))
                wait(dve, negmax_T, h.times(1, -1))
                dve.tensor_scalar(negmax[:, h.parity, :, 0], rowmax[:, h.parity, :], -1.0, None, ALU.mult)\
                    .then_inc(negmax_chain, 1)

            def negmax_low(h):
                dve.wait_ge(negmax_chain, h.times(1, 1))
                dve.scalar_tensor_tensor(negmax[:, h.parity, :, 1], rowmax[:, h.parity, :], -1.0,
                                         negmax[:, h.parity, :, 0], ALU.mult, ALU.subtract)\
                    .then_inc(negmax_ready, 1)

            def stacks(h):
                dve.wait_ge(stack_T, h.times(1, 1))
                wait(dve, shifted_done, h.times(1, -1))
                dve.tensor_copy(qk[0:STACK, h.parity, :, :].rearrange("p a t -> p (a t)"),
                                bank16(0)[0:STACK, :]).then_inc(stack_ready, 1)

            def negmax_rows(h):
                dve.wait_ge(negmax_T, h.times(1, 1))
                wait(dve, shifted_done, h.times(1, -1))
                dve.tensor_copy(qk[STACK:P, h.parity, 0, :], bank16(0)[STACK:P, 0:SEQ])\
                    .then_inc(negmax_stacked, 1)

            def sum_inverse(h):
                dve.wait_ge(pv_done, h.times(1, 1))
                wait(dve, o_stored, h.times(1, 0))
                dve.reciprocal(rsum[:, :], pv[:, :, HD]).then_inc(rsum_ready, 1)

            def normalise(h):
                dve.wait_ge(rsum_ready, h.times(1, 1))
                dve.tensor_tensor(ost[:, bass.ds(h.times(1), 1), :, :].rearrange("p a s c -> p (a s) c"),
                                  pv[:, :, 0:HD],
                                  rsum[:, :].unsqueeze(2).to_broadcast([P, SEQ_TILES, HD]), ALU.mult)\
                    .then_inc(o_stored, 1)

            pipelined(dve, UNITS, 2, [(1, maxima), (0, stacks), (1, negmax_high), (4, sum_inverse), (1, negmax_low), (4, normalise), (1, negmax_rows)], peel=6)
            dve.wait_ge(o_stored, UNITS)
            dve.sem_inc(attended, 1)

            def x1(t):
                st = small[:, t.parity, 32:]
                arrived(dve, o_x_in, t)
                dve.wait_ge(o_y_ln, t.times(1, 1))
                wait(dve, o_x1_rstd, t.times(1, -1))
                dve.tensor_tensor(heads_of(t, ost, 0, HD), by_head(o_y[:, t.parity, :]),
                                  by_head(o_x[:, t.parity, :]), ALU.add).then_inc(o_x1_chain, 1)
                wait_apart(dve, o_x1_chain, t.times(2, 1), tally)
                dve.bn_stats(st[:, 0:6], heads_of(t, ost, 0, HD)).then_inc(o_x1_chain, 1)
                wait_apart(dve, o_x1_chain, t.times(2, 2), tally)
                dve.bn_aggr(st[:, 6:8], st[:, 0:6]).then_inc(o_x1_stats, 1)

            def y(t):
                st = small[:, t.parity, :]
                dve.wait_ge(o_proj_done, t.times(1, 1))
                wait(dve, o_y_rstd, t.times(1, -1))
                dve.tensor_tensor(o_y[:, t.parity, :], bank(1 + t.parity), bo_all[:, :], ALU.add)\
                    .then_inc(o_y_chain, 1)
                dve.wait_ge(o_y_chain, t.times(2, 1))
                dve.bn_stats(st[:, 0:6], o_y[:, t.parity, :]).then_inc(o_y_chain, 1)
                wait_apart(dve, o_y_chain, t.times(2, 2), tally)
                dve.bn_aggr(st[:, 6:8], st[:, 0:6]).then_inc(o_y_stats, 1)

            def x2(t):
                st = small[:, t.parity, 32:]
                dve.wait_ge(o_x1_rstd, t.times(1, 1))
                wait(dve, o_lo_ready, t.times(1, 0))
                dve.tensor_scalar(by_head(o_x2), heads_of(t, ost, 0, HD), st[:, 9:10], st[:, 10:11],
                                  ALU.mult, ALU.add).then_inc(o_x2_ready, 1)

            dve.wait_ge(attended, 4)
            pipelined(dve, TILES, 4, [(2, x1), (1, y), (2, x2)])
            dve.wait_ge(o_x2_ready, TILES)
            dve.sem_inc(mixed, 1)

            dve.wait_ge(mixed, 4)
            dve.sem_inc(fuse_ready, PRIMED)
            dve.sem_inc(y_read, PRIMED)
            dve.sem_inc(out_ready, 1)
            with dve.Fori(0, BATCH) as c:
                with dve.Fori(0, ITILES // 2) as j:
                    for u in range(2):
                        i = j * 2 + u
                        n = c * ITILES + i
                        dve.wait_ge(up_done, n + 1)
                        dve.wait_ge(silu_ready, n + (1 + PRIMED))
                        dve.wait_ge(flo_ready, n + 1)
                        dve.scalar_tensor_tensor(f_prod[:, u, :], bank(2 + u), sup[:, bass.ds(i, 1)],
                                                 f_silu[:, u, :], ALU.mult, ALU.mult).then_inc(fuse_ready, 1)

                def add_residual(u):
                    t = c * CTILES + u
                    dve.wait_ge(y_ln, t + (1 + PRIMED))
                    dve.tensor_tensor(by_head(f_out[:, u, :]), by_head(f_y[:, u % 2, :]),
                                      ost[:, bass.ds(c * HEADS, HEADS), u, :], ALU.add).then_inc(out_ready, 1)

                dve.wait_ge(chunk_stored, c + 1)
                for u in range(CTILES):
                    t = c * CTILES + u
                    st = small[:, u % 2, :]
                    dve.wait_ge(out_ready, c * CTILES + (max(u - 1, 0) + 1))
                    dve.wait_ge(down_done, t + 2)
                    dve.tensor_tensor(f_y[:, u % 2, :], bank(4 + u % 2), sdown[:, :], ALU.mult)\
                        .then_inc(y_read, 1)
                    dve.wait_ge(y_read, t + (1 + PRIMED))
                    dve.bn_stats(st[:, 0:6], f_y[:, u % 2, :]).then_inc(y_chain, 1)
                    wait_apart(dve, y_chain, t + 1, tally)
                    dve.bn_aggr(st[:, 6:8], st[:, 0:6]).then_inc(y_stats, 1)
                    if u:
                        add_residual(u - 1)
                add_residual(CTILES - 1)

        @block.tensor
        def _(pe):
            def transposes(n, src, ident_, name):
                for g in range(GROUPS):
                    last = pe.transpose(PS[:, n, P * g:P * g + P], src(g), ident_)
                last.then_inc(setup_pe, 1)

            def products(n, lhs, rhs, name):
                for g in range(GROUPS):
                    last = pe.matmul(PS[:, n, P * g:P * g + P], lhs(g), rhs(g), start=True, stop=True)
                last.then_inc(setup_pe, 1)

            def tile_of(m):
                return lambda g: m[:, P * g:P * g + P]

            def group_of(m):
                return lambda g: m[:, g, :]

            pe.wait_ge(setup_dve, nth(SETUP_DVE, "ones"))
            pe.wait_ge(wdkv_in, 16)
            pe.matmul(bank(0), ones[:, :], wdkv_sb, start=True, stop=True).then_inc(setup_pe, 1)
            pe.wait_ge(consts_ready, 9)
            pe.wait_ge(heads_in, 32)
            transposes(1, tile_of(wuk_sb), ident[:, :], "wukT")
            transposes(2, tile_of(wuv_sb), ident[:, :], "wuvT")
            pe.wait_ge(vecs_in, 64)
            pe.transpose(PS[:, 5, 0:64], vec_rows[0:64, :], ident[0:64, 0:64]).then_inc(setup_pe, 1)
            pe.wait_ge(blockdiag_in, 128)
            transposes(3, group_of(bdq), ident[:, :], "bdqT")
            transposes(4, group_of(bdo), ident[:, :], "bdoT")
            pe.wait_ge(setup_dve, nth(SETUP_DVE, "bdqT"))
            products(6, group_of(wukT), group_of(bdqT), "A")
            pe.wait_ge(setup_act, nth(SETUP_ACT, "bdoT"))
            products(7, group_of(wuvT), group_of(bdoT), "U")
            products(0, tile_of(wc), tile_of(wc), "G")
            pe.wait_ge(setup_dve, nth(SETUP_DVE, "gA"))
            products(1, tile_of(wc), tile_of(gA), "M")
            pe.wait_ge(setup_dve, nth(SETUP_DVE, "gU"))
            products(2, tile_of(wc), tile_of(gU), "N")
            pe.wait_ge(setup_dve, nth(SETUP_DVE, "absA"))
            pe.matmul(bank(6), ones[:, :], absA, start=True, stop=True).then_inc(setup_pe, 1)
            pe.matmul(bank(4), ones[:, :], bA, start=True, stop=True).then_inc(setup_pe, 1)
            pe.wait_ge(setup_dve, nth(SETUP_DVE, "bU"))
            products(5, tile_of(bU), lambda g: ones[:, :], "vb")
            pe.wait_ge(setup_dve, nth(SETUP_DVE, "absU"))
            pe.matmul(bank(7), ones[:, :], absU, start=True, stop=True).then_inc(setup_pe, 1)
            pe.wait_ge(wo_in, 16)
            pe.wait_ge(setup_dve, nth(SETUP_DVE, "bounds"))
            for k in range(GROUPS):
                if k >= 2:
                    pe.wait_ge(setup_act, nth(SETUP_ACT, f"woT{k - 2}"))
                transposes(6 + k % 2, lambda g: wo_nat[:, g, P * k:P * k + P], ident[:, :], f"woT{k}")
            pe.wait_ge(setup_dve, nth(SETUP_DVE, "fusemax"))
            pe.transpose(bank(3)[0:1, 0:P], scratch[:, 16:17], ident[:, :]).then_inc(setup_pe, 1)
            pe.wait_ge(setup_dve, nth(SETUP_DVE, "fusered"))
            pe.matmul(bank(3)[:, 0:1], ones[0:1, :], scratch[0:1, 17:18], start=True, stop=True)\
                .then_inc(setup_pe, 1)
            pe.wait_ge(setup_act, nth(SETUP_ACT, "woT3"))
            for g in range(GROUPS):
                last = pe.matmul(bank(5), vb_sb[:, g, :], WoT[:, g, :], start=(g == 0), stop=(g == GROUPS - 1))
            last.then_inc(setup_pe, 1)

            def keys_values(t):
                wait(pe, p_value_ready, t.times(1, -1))
                for m, n in ((1, 4), (2, 6)):
                    for g in range(GROUPS):
                        last = pe.matmul(PS[:, n + t.parity, P * g:P * g + P], p_xT[:, t.parity, g, :],
                                         GMN[:, g, m, :], start=True, stop=True)
                last.then_inc(p_MN_done, 1)

            def variance(t):
                pe.wait_ge(p_prod_ready, t.times(1, 1))
                wait(pe, p_var_eps, t.times(1, 0))
                for g in range(GROUPS):
                    last = pe.matmul(bank(3)[:, GH * g:GH * g + GH], p_prod[:, t.parity, g, :], headsum[:, :],
                                     start=True, stop=True)
                last.then_inc(p_var_done, 1)

            def xln_T(t):
                pe.wait_ge(p_ln_ready, t.times(1, 1))
                wait(pe, p_xT_ready, t.times(1, 0))
                for g in range(GROUPS):
                    last = pe.transpose(PS[:, 0, P * g:P * g + P], p_ln[:, t.slot, P * g:P * g + P],
                                        ident[:, :])
                last.then_inc(p_T_done, 1)

            def gram(t):
                pe.wait_ge(p_xT_ready, t.times(1, 1))
                wait(pe, p_prod_ready, t.times(1, 0))
                for g in range(GROUPS):
                    last = pe.matmul(PS[:, 1, P * g:P * g + P], GMN[:, g, 0, :], p_xT[:, t.parity, g, :],
                                     start=True, stop=True)
                last.then_inc(p_G_done, 1)

            pe.wait_ge(setup_dve, nth(SETUP_DVE, "done"))
            pipelined(pe, TILES, 4, [(2, keys_values), (1, xln_T), (2, variance), (1, gram)], peel=8)
            pe.wait_ge(p_MN_done, TILES)
            pe.wait_ge(p_var_done, TILES)
            pe.sem_inc(projected, 1)

            def scores(h):
                pe.wait_ge(stack_ready, h.times(1, 1))
                wait(pe, max_done, h.times(1, 0))
                for s, (n, at) in enumerate(SCORE_AT):
                    last = pe.matmul(PS[:, n, at:at + (s + 1) * P], qk[0:STACK, h.parity, 0, P * s:P * s + P],
                                     qk[0:STACK, h.parity, 1, 0:(s + 1) * P], start=True, stop=True)
                last.then_inc(scores_done, 1)

            def shifted(h):
                pe.wait_ge(negmax_stacked, h.times(1, 1))
                wait(pe, prob_ready, h.times(1, 0))
                for t, (n, at) in enumerate(SHIFTED_AT):
                    pe.matmul(PS[:, n, at:at + SEQ - P * t], qk[:, h.parity, 1, P * t:P * t + P],
                              qk[:, h.parity, 0, P * t:SEQ], start=True, stop=False)
                    last = pe.matmul(PS[:, n, at:at + P], identb[:, :], causalT[:, :], start=False, stop=True)
                last.then_inc(shifted_done, 1)

            def weighted(h):
                pe.wait_ge(prob_lo_ready, h.times(1, 1))
                wait(pe, o_stored, h.times(1, 0))
                for s in range(SEQ_TILES):
                    for t in range(s + 1):
                        at = PROB_AT[t] + P * (s - t)
                        v = vst[:, bass.ds(h.times(1), 1), t, :].rearrange("p a c -> p (a c)")
                        for n, (part, lo) in enumerate(((0, 0), (0, VH), (1, 0))):
                            last = pe.matmul(pv[:, s, :],
                                             prob_parts[:, h.parity, part, at:at + P], v[:, lo:lo + VH],
                                             start=(t == 0 and n == 0), stop=(t == s and n == 2))
                last.then_inc(pv_done, 1)

            def stack_transposes(h):
                wait(pe, stack_ready, h.times(1, 0))
                for a, stack in enumerate((qst, kst)):
                    for s in range(SEQ_TILES):
                        last = pe.transpose(bank16(0)[0:STACK, SEQ * a + P * s:SEQ * a + P * s + P],
                                            stack[:, bass.ds(h.times(1), 1), s, :].rearrange("p a c -> p (a c)"),
                                            ident16[:, :])
                last.then_inc(stack_T, 1)

            def negmax_transposes(h):
                pe.wait_ge(negmax_ready, h.times(1, 1))
                wait(pe, negmax_stacked, h.times(1, 0))
                for s in range(SEQ_TILES):
                    last = pe.transpose(bank16(0)[STACK:P, P * s:P * s + P], negmax[:, h.parity, s, :],
                                        ident16[:, :])
                last.then_inc(negmax_T, 1)

            pe.wait_ge(projected, 4)
            pe.wait_ge(key_rows, 2)
            pipelined(pe, UNITS, 2, [(1, scores), (2, shifted), (0, stack_transposes), (4, weighted), (1, negmax_transposes)], peel=6)
            pe.wait_ge(pv_done, UNITS)
            pe.sem_inc(attended, 1)

            def project(t):
                pe.wait_ge(o_T_ready, t.times(1, 1))
                wait(pe, o_y_stats, t.times(1, -1))
                for g in range(GROUPS):
                    last = pe.matmul(bank(1 + t.parity), o_T[:, t.parity, g, :], WoT[:, g, :],
                                     start=(g == 0), stop=(g == GROUPS - 1))
                last.then_inc(o_proj_done, 1)

            def o_transposes(t):
                pe.wait_ge(o_staged, t.times(1, 1))
                wait(pe, o_T_ready, t.times(1, 0))
                for g in range(GROUPS):
                    last = pe.transpose(PS[:, 0, P * g:P * g + P], o_in[:, t.parity, P * g:P * g + P],
                                        ident[:, :])
                last.then_inc(o_T_done, 1)

            def x2_transposes(t):
                pe.wait_ge(o_lo_ready, t.times(1, 1))
                wait(pe, o_x2T_ready, t.times(1, 0))
                for part in range(2):
                    for k in range(GROUPS):
                        at = P * (part * GROUPS + k)
                        last = pe.transpose(bank16(3)[:, at:at + P], o_parts[:, t.parity, part, P * k:P * k + P],
                                            ident16[:, :])
                last.then_inc(o_x2T_done, 1)

            pe.wait_ge(attended, 4)
            pipelined(pe, TILES, 4, [(1, project), (0, o_transposes), (3, x2_transposes)])
            pe.wait_ge(o_x2T_done, TILES)
            pe.sem_inc(mixed, 1)

            pe.wait_ge(mixed, 4)
            pe.wait_ge(wffn_in, 48)
            pe.sem_inc(down_done, 1)
            with pe.Fori(0, BATCH) as c:
                with pe.Fori(0, ITILES // 2) as j:
                    for u in range(2):
                        i = j * 2 + u
                        n = c * ITILES + i
                        for m, free, done in ((0, silu_ready, gate_done), (1, fuse_ready, up_done)):
                            pe.wait_ge(free, n + 1)
                            for k in range(GROUPS):
                                for part in range(2):
                                    last = pe.matmul(
                                        bank(2 * m + u), w_gu[:, m, k, bass.ds(i * P, P)],
                                        x2T[:, part * GROUPS + k, bass.ds(c * CHUNK, CHUNK)],
                                        start=(k == 0 and part == 0), stop=(k == GROUPS - 1 and part == 1))
                            last.then_inc(done, 1)
                for u in range(CTILES):
                    t = c * CTILES + u
                    pe.wait_ge(y_read, t + 1)
                    for i in range(ITILES):
                        if u == 0 and i in (0, ITILES - 2, ITILES - 1):
                            pe.wait_ge(flo_ready, c * ITILES + (max(i + 1, ITILES - 2) + PRIMED))
                        for part in range(2):
                            last = pe.matmul(bank(4 + u % 2), fused[:, part, i, P * u:P * u + P], w_dn[:, i, :],
                                             start=(i == 0 and part == 0), stop=(i == ITILES - 1 and part == 1))
                    last.then_inc(down_done, 1)


_INS = ["L0_attn_x", "L0_attn_Wq", "L0_attn_Wdkv", "L0_attn_Wuk", "L0_attn_Wuv", "L0_attn_ln_g", "L0_attn_ln_b",
        "L0_attn_Wo_h", "L0_attn_Wo", "L0_attn_bo", "L0_ffn_w_gate", "L0_ffn_w_up", "L0_ffn_w_down",
        "L0_ffn_s_gate", "L0_ffn_s_up", "L0_ffn_s_down"]


def kernel(**inputs):
    import numpy as np
    import concourse.bacc as bacc
    from concourse.bass_utils import run_bass_kernel_spmd

    nc = bacc.Bacc("TRN2", target_bir_lowering=False, num_devices=1)
    arrays, args = {}, []
    for name in _INS:
        a = np.ascontiguousarray(inputs[name])
        if a.dtype.itemsize == 1:
            a = a.view(np.int32)
        arrays[f"in_{name}"] = a
        args.append(nc.dram_tensor(f"in_{name}", a.shape, mybir.dt.from_np(a.dtype), kind="ExternalInput").ap())
    args.append(nc.dram_tensor("out_x", (BATCH, SEQ, EMB), mybir.dt.float32, kind="ExternalOutput").ap())
    block_kernel(nc, *args)
    r = run_bass_kernel_spmd(nc, [arrays], core_ids=[0])
    return r.results[0]["out_x"]
```

```python
import math
from contextlib import ExitStack

import concourse.bass as bass
from concourse import mybir

P = 128
BATCH, SEQ, EMB = 4, 512, 512
HEADS, HD, LAT = 16, 32, 128
INTER = 2048
TOKENS = BATCH * SEQ
TILES = TOKENS // P
SEQ_TILES = SEQ // P
UNITS = BATCH * HEADS
GROUPS = EMB // P
GH = P // HD
ITILES = INTER // P
CHUNK = 512
CTILES = CHUNK // P
STACK = 3 * HD
EPS = 1e-5
VH = HD + 1
VW = 2 * VH
X2_SCALE = 2048.0
KEY_BOUND = 256.0
VALUE_BOUND = 2048.0
LATENT_MAX = 11.5
FUSE_BOUND = 32000.0
RAW_BOUND = 2.0 ** 16
NEG = -1e30
EARLY = 2

SETUP_PE = ["mean", "wukT", "wuvT", "vecT", "bdqT", "bdoT", "A", "U", "G", "keybound", "valuebound", "M", "N",
            "keybias", "vb", "woT0", "woT1", "woT2", "woT3", "fuseT", "bo", "fuseall"]
SETUP_DVE = ["ones", "bdzero", "gmnzero", "Wc", "wukT", "vecT", "bdqT", "absA", "absU", "gA", "gU", "bounds",
             "M", "N", "bA", "bU", "keybias", "vb", "fusemax", "done", "fusered", "fusebound"]
SETUP_ACT = ["wuvT", "bdoT", "G", "woT0", "woT1", "woT2", "woT3", "bo"]


def nth(order, name):
    return order.index(name) + 1


class Step:

    def __init__(self, unit, loop, const):
        self.unit, self.loop, self.const = unit, loop, const

    def minus(self, lag):
        return Step(self.unit, self.loop, self.const - lag)

    def times(self, k, plus=0):
        whole = k * self.const + plus
        return whole if self.loop is None else self.loop * (k * self.unit) + whole

    @property
    def parity(self):
        return self.const % 2

    @property
    def slot(self):
        return self.const % 4

    @property
    def batch(self):
        q = self.const // self.unit
        return q if self.loop is None else self.loop + q

    @property
    def sub(self):
        return self.const % self.unit


def wait(eng, sem, value):
    if isinstance(value, int) and value <= 0:
        return
    eng.wait_ge(sem, value)


def wait_apart(eng, sem, value, tally):
    if isinstance(value, int) and value <= 0:
        return
    eng.wait_ge(sem, value)
    eng.sem_inc(tally, 1)


def pipelined(eng, n, unit, stages, peel=4):
    deepest = max(lag for lag, _ in stages)

    def step(s, base):
        for lag, fn in stages:
            at = s.minus(lag)
            if base is None or 0 <= base - lag < n:
                fn(at)

    for s in range(peel):
        step(Step(unit, None, s), s)
    with eng.Fori(peel // unit, n // unit) as loop:
        for u in range(unit):
            step(Step(unit, loop, u), None)
    for s in range(n, n + deepest):
        step(Step(unit, None, s), s)


def block_kernel(nc, x, Wq, Wdkv, Wuk, Wuv, ln_g, ln_b, Wo_h, Wo, bo, w_gate, w_up, w_down,
                 s_gate, s_up, s_down, out):
    f32, f16, bf16 = mybir.dt.float32, mybir.dt.float16, mybir.dt.bfloat16
    ALU, ACT, AX = mybir.AluOpType, mybir.ActivationFunctionType, mybir.AxisListType
    ctx = ExitStack()
    with ctx:
        def sb(name, shape, dt):
            return ctx.enter_context(nc.sbuf_tensor(name, shape, dt))

        def sem(name):
            return ctx.enter_context(nc.semaphore(name))

        ident = sb("ident", [P, P], f32)
        ident16 = sb("ident16", [P, P], f16)
        identb = sb("identb", [P, P], bf16)
        causalT = sb("causalT", [P, P], bf16)
        ones = sb("ones", [P, P], f32)
        headsum = sb("headsum", [P, GH], f32)
        halfneg = sb("halfneg", [P, 1], f32)
        vec = sb("vec", [P, 4 * HEADS], f32)
        sgate = sb("sgate", [P, ITILES], f32)
        sup = sb("sup", [P, ITILES], f32)
        kscale = sb("kscale", [P, 5], f32)
        small = sb("small", [P, 4, 96], f32)
        negmax = sb("negmax", [P, 2, SEQ_TILES, HD], f16)
        rowmax = sb("rowmax", [P, 2, SEQ_TILES], f32)
        rsum = sb("rsum", [P, SEQ_TILES], f32)
        scratch = sb("scratch", [P, 64], f32)
        GMN = sb("GMN", [P, GROUPS, 3, P], f32)
        keybias = sb("keybias", [P, EMB], f32)
        WoT = sb("WoT", [P, GROUPS, EMB], f32)
        bo_all = sb("bo_all", [P, EMB], f32)
        sdown = sb("sdown", [P, EMB], f32)
        TMP = sb("TMP", [P, 10 * EMB], f32)
        Q = sb("Q", [P, UNITS * SEQ_TILES * STACK], f16)
        K = sb("K", [P, UNITS * SEQ_TILES * STACK], f16)
        V = sb("V", [P, UNITS * SEQ_TILES * VW], f16)
        O = sb("O", [P, UNITS * SEQ_TILES * HD], f32)
        qst = Q[:, :].rearrange("p (n s c) -> p n s c", s=SEQ_TILES, c=STACK)
        kst = K[:, :].rearrange("p (n s c) -> p n s c", s=SEQ_TILES, c=STACK)
        vst = V[:, :].rearrange("p (n s c) -> p n s c", s=SEQ_TILES, c=VW)
        ost = O[:, :].rearrange("p (n s c) -> p n s c", s=SEQ_TILES, c=HD)

        def carve(t, start, shape, dt=f32):
            n = math.prod(shape)
            words = n if dt == f32 else n // 2
            v = t[:, start:start + words] if t.dtype == f32 else t[:, 2 * start:2 * (start + words)].bitcast(f32)
            v = v if dt == f32 else v.bitcast(dt)
            names = "abcd"[:len(shape)]
            return v.rearrange(f"p ({' '.join(names)}) -> p {' '.join(names)}",
                               **{k: s for k, s in zip(names[1:], shape[1:])}) if len(shape) > 1 else v

        wdkv_sb = carve(O, 0, [EMB])
        wuk_sb = carve(O, 512, [EMB])
        wuv_sb = carve(O, 1024, [EMB])
        bdq = carve(O, 1536, [GROUPS, P])
        bdo = carve(O, 2048, [GROUPS, P])
        wo_nat = carve(O, 2560, [GROUPS, EMB])
        bdqT = carve(O, 4608, [GROUPS, P])
        bdoT = carve(O, 5120, [GROUPS, P])
        wukT = carve(O, 5632, [GROUPS, P])
        wuvT = carve(O, 6144, [GROUPS, P])
        wc = carve(O, 6656, [EMB])
        vb_sb = carve(O, 7168, [GROUPS, P])
        vec_rows = carve(O, 7680, [P])
        gA, bA, absA, gU, bU, absU = (carve(V, EMB * n, [EMB]) for n in range(6))
        p_x = carve(TMP, 0, [4, EMB])
        p_ln = carve(TMP, 2048, [4, EMB])
        p_xT = carve(TMP, 4096, [2, GROUPS, P])
        p_prod = carve(O, 0, [2, GROUPS, P])
        p_key = carve(O, 1024, [4, EMB])
        p_value = carve(O, 3072, [4, EMB])
        gmn_flat = GMN[:, :, :, :].rearrange("p g m c -> p (g m c)")
        prob = carve(TMP, 0, [2, 1280])
        prob_parts = carve(TMP, 2560, [2, 2, 1280], f16)
        qk = gmn_flat[:, 0:1024].bitcast(f16).rearrange("p (b a t) -> p b a t", b=2, a=2)
        causal = gmn_flat[:, 1024:1024 + SEQ]
        o_x = carve(TMP, 0, [4, EMB])
        o_in = carve(TMP, 2048, [2, EMB])
        o_T = carve(TMP, 3072, [2, GROUPS, P])
        o_y = carve(K, 8192, [4, EMB])
        o_x2 = carve(K, 10240, [4, EMB])
        o_parts = gmn_flat[:, 0:2 * EMB].bitcast(f16).rearrange("p (b h c) -> p b h c", b=2, h=2)
        w_gu = V[:, 0:2 * GROUPS * INTER].rearrange("p (m k n) -> p m k n", m=2, k=GROUPS)
        x2T = K[:, 0:2 * GROUPS * TOKENS].rearrange("p (h k t) -> p (h k) t", h=2, k=GROUPS)
        fused = Q[:, 0:2 * ITILES * CHUNK].rearrange("p (h i t) -> p h i t", h=2, i=ITILES)
        w_dn = Q[:, 2 * ITILES * CHUNK:3 * ITILES * CHUNK].rearrange("p (i n) -> p i n", i=ITILES)
        f_silu = carve(TMP, 0, [2, CHUNK])
        f_prod = carve(TMP, 1024, [2, CHUNK])
        f_y = carve(TMP, 2048, [2, EMB])
        f_out = WoT[:, :, :]

        SCORE_ORDER = (3, 1, 2, 0)
        SCORE_AT = [(2, 384), (3, 0), (2, 0), (1, 0)]
        SHIFTED_AT = [(4, 0), (5, 0), (6, 0), (5, 384)]
        PROB_AT = [0, 512, 1024, 896]

        PS = ctx.enter_context(nc.psum_tensor("PS", [P, 8, 512], f32))

        def bank(n):
            return PS[:, n, :]

        def bank16(n):
            return PS[:, n, :].bitcast(f16)

        pv = PS[:, 7, 0:SEQ_TILES * VH].rearrange("p (s c) -> p s c", c=VH)

        def diagonal(n, rows):
            return PS[rows, n, :].rearrange("p (g c) -> p g c", c=P)[:, :, rows]

        def by_head(ap):
            return ap.rearrange("p (h c) -> p h c", c=HD)

        tally = sem("tally")
        consts_ready = sem("consts_ready")
        wdkv_in = sem("wdkv_in")
        heads_in = sem("heads_in")
        vecs_in = sem("vecs_in")
        blockdiag_in = sem("blockdiag_in")
        wo_in = sem("wo_in")
        rows_in = sem("rows_in")
        setup_pe = sem("setup_pe")
        setup_dve = sem("setup_dve")
        setup_act = sem("setup_act")
        setup_chain = sem("setup_chain")
        p_x_in = [sem(f"p_x_in{n}") for n in range(4)]
        p_stats_chain = sem("p_stats_chain")
        p_stats = sem("p_stats")
        p_rstd = sem("p_rstd")
        p_shift = sem("p_shift")
        p_ln_ready = sem("p_ln_ready")
        p_hi_ready = sem("p_hi_ready")
        p_lo_ready = sem("p_lo_ready")
        p_T_done = sem("p_T_done")
        p_xT_ready = sem("p_xT_ready")
        p_G_done = sem("p_G_done")
        p_MN_done = sem("p_MN_done")
        p_prod_ready = sem("p_prod_ready")
        p_var_done = sem("p_var_done")
        p_var_eps = sem("p_var_eps")
        p_root_ready = sem("p_root_ready")
        p_newton_chain = sem("p_newton_chain")
        p_key_raw = sem("p_key_raw")
        p_key_ready = sem("p_key_ready")
        p_khi_ready = sem("p_khi_ready")
        p_klo_ready = sem("p_klo_ready")
        p_value_ready = sem("p_value_ready")
        p_vhi_ready = sem("p_vhi_ready")
        p_vlo_ready = sem("p_vlo_ready")
        projected = sem("projected")
        att_consts = sem("att_consts")
        key_rows = sem("key_rows")
        att_mask = sem("att_mask")
        stack_T = sem("stack_T")
        stack_ready = sem("stack_ready")
        scores_done = sem("scores_done")
        max_done = sem("max_done")
        negmax_chain = sem("negmax_chain")
        negmax_ready = sem("negmax_ready")
        negmax_T = sem("negmax_T")
        negmax_stacked = sem("negmax_stacked")
        shifted_done = sem("shifted_done")
        prob_ready = sem("prob_ready")
        prob_hi_ready = sem("prob_hi_ready")
        prob_lo_ready = sem("prob_lo_ready")
        pv_done = sem("pv_done")
        rsum_ready = sem("rsum_ready")
        o_stored = sem("o_stored")
        attended = sem("attended")
        o_x_in = [sem(f"o_x_in{n}") for n in range(4)]
        o_staged = sem("o_staged")
        o_T_done = sem("o_T_done")
        o_T_ready = sem("o_T_ready")
        o_proj_done = sem("o_proj_done")
        o_y_raw = sem("o_y_raw")
        o_y_chain = sem("o_y_chain")
        o_y_stats = sem("o_y_stats")
        o_y_rstd = sem("o_y_rstd")
        o_y_shift = sem("o_y_shift")
        o_y_ln = sem("o_y_ln")
        o_x1_raw = sem("o_x1_raw")
        o_x1_chain = sem("o_x1_chain")
        o_x1_stats = sem("o_x1_stats")
        o_x1_rstd = sem("o_x1_rstd")
        o_x1_shift = sem("o_x1_shift")
        o_x2_ready = sem("o_x2_ready")
        o_hi_ready = sem("o_hi_ready")
        o_lo_ready = sem("o_lo_ready")
        o_x2T_done = sem("o_x2T_done")
        o_x2T_ready = sem("o_x2T_ready")
        wffn_in = sem("wffn_in")
        mixed = sem("mixed")
        gate_done = sem("gate_done")
        up_done = sem("up_done")
        silu_ready = sem("silu_ready")
        fuse_ready = sem("fuse_ready")
        fhi_ready = sem("fhi_ready")
        flo_ready = sem("flo_ready")
        down_done = sem("down_done")
        y_read = sem("y_read")
        y_chain = sem("y_chain")
        y_stats = sem("y_stats")
        y_pool = sem("y_pool")
        y_rstd = sem("y_rstd")
        y_ln = sem("y_ln")
        out_ready = sem("out_ready")
        chunk_stored = sem("chunk_stored")
        out_stored = sem("out_stored")
        PRIMED = 2

        w_gate, w_up, w_down = (w.bitcast(mybir.dt.int8) for w in (w_gate, w_up, w_down))
        x_tiles = x.rearrange("b (s p) e -> p (b s) e", p=P)
        out_tiles = out.rearrange("b (s p) e -> p (b s) e", p=P)

        def heads_of(t, stack, lo, hi):
            return stack[:, bass.ds(t.batch * HEADS, HEADS), t.sub, lo:hi]

        def arrived(eng, sems, t):
            eng.wait_ge(sems[t.slot], (t.batch + 1) * 16)

        def across(r):
            return r.unsqueeze(2).to_broadcast([P, HEADS, HD])

        block = ctx.enter_context(nc.Block())

        @block.sync
        def _(sp):
            sp.dma_start(by_head(wdkv_sb), Wdkv.rearrange("h l d -> l h d")).then_inc(wdkv_in, 16)
            sp.dma_start(by_head(wuk_sb), Wuk.rearrange("h l d -> l h d")).then_inc(heads_in, 16)
            sp.dma_start(by_head(wuv_sb), Wuv.rearrange("h l d -> l h d")).then_inc(heads_in, 16)
            for n, v in enumerate((ln_g, ln_b, s_gate.rearrange("(c p) -> c p", p=P),
                                   s_up.rearrange("(c p) -> c p", p=P))):
                sp.dma_start(vec_rows[16 * n:16 * n + 16, :], v).then_inc(vecs_in, 16)
            sp.wait_ge(setup_dve, nth(SETUP_DVE, "bdzero"))
            for a in range(GH):
                for dst, w in ((bdq, Wq), (bdo, Wo_h)):
                    sp.dma_start(dst[HD * a:HD * a + HD, :, HD * a:HD * a + HD],
                                 w.rearrange("(g a) i j -> a i g j", a=GH)[a]).then_inc(blockdiag_in, 16)
            sp.dma_start(wo_nat, Wo.rearrange("(m p) n -> p m n", p=P)).then_inc(wo_in, 16)
            sp.dma_start(bo_all[:, :], bo.partition_broadcast(P)).then_inc(rows_in, 16)
            sp.dma_start(sdown[:, :], s_down.partition_broadcast(P)).then_inc(rows_in, 16)

            def load_x(dst, buffer, sems, t):
                sp.dma_start(dst[:, buffer, :], x_tiles[:, bass.ds(t.times(1), 1), :]
                             .rearrange("p a e -> p (a e)")).then_inc(sems[t.slot], 16)

            def load_p_x(t):
                wait(sp, p_ln_ready, t.times(1, -3))
                load_x(p_x, t.slot, p_x_in, t)

            def load_o_x(t):
                wait(sp, o_x1_raw, t.times(1, -3))
                load_x(o_x, t.slot, o_x_in, t)

            pipelined(sp, TILES, 4, [(0, load_p_x)])
            sp.wait_ge(attended, 4)
            pipelined(sp, TILES, 4, [(0, load_o_x)])
            sp.sem_inc(chunk_stored, 1)
            with sp.Fori(0, BATCH) as c:
                for u in range(CTILES):
                    sp.wait_ge(out_ready, c * CTILES + (u + 2))
                    sp.dma_start(out_tiles[:, bass.ds(c * CTILES + u, 1), :].rearrange("p a e -> p (a e)"),
                                 f_out[:, u, :]).then_inc(out_stored, 16)
                sp.wait_ge(out_stored, (c + 1) * (16 * CTILES))
                sp.sem_inc(chunk_stored, 1)
            sp.wait_ge(out_stored, 16 * TILES)

        @block.gpsimd
        def _(pool):
            for m, v in ((ident, 0.0), (ident16, 0.0), (identb, 0.0), (causalT, 0.0), (halfneg, -0.5)):
                pool.memset(m[:, :], v).then_inc(consts_ready, 1)
            pool.wait_ge(consts_ready, 5)
            for m in (ident, ident16, identb):
                pool.affine_select(out=m[:, :], in_=m[:, :], compare_op=ALU.not_equal, fill=1.0, base=0,
                                   pattern=[[-1, P]], channel_multiplier=1).then_inc(consts_ready, 1)
            pool.affine_select(out=causalT[:, :], in_=causalT[:, :], compare_op=ALU.is_ge, fill=NEG, base=0,
                               pattern=[[1, P]], channel_multiplier=-1).then_inc(consts_ready, 1)

            def x_scale(t):
                st = small[:, t.slot, :]
                pool.wait_ge(p_stats, t.times(1, 1))
                pool.tensor_tensor(st[:, 9:10], st[:, 8:9], halfneg[:, :], ALU.pow).then_inc(p_rstd, 1)

            def x_low(t):
                pool.wait_ge(p_hi_ready, t.times(1, 1))
                pool.tensor_tensor(heads_of(t, qst, HD, 2 * HD), by_head(p_ln[:, t.slot, :]),
                                   heads_of(t, qst, 0, HD), ALU.subtract).then_inc(p_lo_ready, 1)

            def key_bias(t):
                pool.wait_ge(p_key_raw, t.times(1, 1))
                pool.tensor_tensor(p_key[:, t.slot, :], p_key[:, t.slot, :], keybias[:, :], ALU.add)\
                    .then_inc(p_key_ready, 1)

            def value_low(t):
                pool.wait_ge(p_vhi_ready, t.times(1, 1))
                pool.tensor_tensor(heads_of(t, vst, VH, VH + HD), by_head(p_value[:, t.slot, :]),
                                   heads_of(t, vst, 0, HD), ALU.subtract).then_inc(p_vlo_ready, 1)

            pool.wait_ge(consts_ready, 9)
            pipelined(pool, TILES, 4, [(2, x_low), (0, x_scale), (4, key_bias), (5, value_low)], peel=8)
            pool.wait_ge(p_vlo_ready, TILES)
            pool.sem_inc(projected, 1)

            pool.wait_ge(projected, 4)
            pool.memset(causal, 0.0).then_inc(att_consts, 1)
            pool.wait_ge(att_consts, 1)
            pool.affine_select(out=causal[:, SEQ - P:], in_=causal[:, SEQ - P:], compare_op=ALU.is_ge, fill=NEG,
                               base=0, pattern=[[-1, P]], channel_multiplier=1).then_inc(att_mask, 1)

            def prob_low(h):
                pool.wait_ge(prob_hi_ready, h.times(1, 1))
                pool.tensor_tensor(prob_parts[:, h.parity, 1, :], prob[:, h.parity, :],
                                   prob_parts[:, h.parity, 0, :], ALU.subtract).then_inc(prob_lo_ready, 1)

            pipelined(pool, UNITS, 8, [(0, prob_low)], peel=8)
            pool.wait_ge(prob_lo_ready, UNITS)
            pool.sem_inc(attended, 1)

            pool.wait_ge(attended, 4)
            for m, w in enumerate((w_gate, w_up)):
                pool.dma_start(w_gu[:, m, :, :], w.rearrange("(k p) n -> p k n", p=P)).then_inc(wffn_in, 16)
            pool.dma_start(w_dn, w_down.rearrange("(i p) n -> p i n", p=P)).then_inc(wffn_in, 16)

            def y_scale(t):
                st = small[:, t.slot, :]
                pool.wait_ge(o_y_stats, t.times(1, 1))
                pool.tensor_tensor(st[:, 9:10], st[:, 8:9], halfneg[:, :], ALU.pow).then_inc(o_y_rstd, 1)

            def x1_scale(t):
                st = small[:, t.slot, 32:]
                pool.wait_ge(o_x1_stats, t.times(1, 1))
                pool.tensor_tensor(st[:, 9:10], st[:, 8:9], halfneg[:, :], ALU.pow).then_inc(o_x1_rstd, 1)

            def x2_low(t):
                pool.wait_ge(o_hi_ready, t.times(1, 1))
                pool.tensor_tensor(o_parts[:, t.parity, 1, :], o_x2[:, t.slot, :], o_parts[:, t.parity, 0, :],
                                   ALU.subtract).then_inc(o_lo_ready, 1)

            pipelined(pool, TILES, 4, [(2, y_scale), (3, x1_scale), (4, x2_low)], peel=8)
            pool.wait_ge(o_lo_ready, TILES)
            pool.sem_inc(mixed, 1)

            pool.wait_ge(mixed, 4)
            pool.sem_inc(flo_ready, PRIMED)
            with pool.Fori(0, BATCH) as c:
                with pool.Fori(0, ITILES // 2) as j:
                    for u in range(2):
                        i = j * 2 + u
                        pool.wait_ge(fhi_ready, c * ITILES + i + (1 + PRIMED))
                        pool.tensor_tensor(fused[:, 1, bass.ds(i, 1), :].rearrange("p a t -> p (a t)"),
                                           f_prod[:, u, :],
                                           fused[:, 0, bass.ds(i, 1), :].rearrange("p a t -> p (a t)"),
                                           ALU.subtract).then_inc(flo_ready, 1)
                for u in range(CTILES):
                    t = c * CTILES + u
                    st = small[:, u % 2, :]
                    wait_apart(pool, y_stats, t + 1, tally)
                    pool.tensor_scalar(st[:, 8:9], st[:, 7:8], EPS, None, ALU.add).then_inc(y_pool, 1)
                    pool.wait_ge(y_pool, t * 2 + 1)
                    pool.wait_ge(y_ln, t + 1)
                    pool.tensor_tensor(st[:, 9:10], st[:, 8:9], halfneg[:, :], ALU.pow).then_inc(y_pool, 1)
                    wait_apart(pool, y_pool, t * 2 + 2, tally)
                    pool.tensor_scalar(st[:, 10:11], st[:, 6:7], st[:, 9:10], -1.0, ALU.mult, ALU.mult)\
                        .then_inc(y_rstd, 1)

        @block.scalar
        def _(act):
            for name, n, dst in (("wuvT", 2, wuvT), ("bdoT", 4, bdoT)):
                act.wait_ge(setup_pe, nth(SETUP_PE, name))
                act.activation(dst.rearrange("p g c -> p (g c)"), bank(n), ACT.Copy).then_inc(setup_act, 1)
            act.wait_ge(setup_dve, nth(SETUP_DVE, "gmnzero"))
            act.wait_ge(setup_pe, nth(SETUP_PE, "G"))
            for a in range(GH):
                rows = slice(HD * a, HD * a + HD)
                last = act.activation(GMN[rows, :, 0, rows], diagonal(0, rows), ACT.Copy, scale=1.0 / LAT)
            last.then_inc(setup_act, 1)
            act.wait_ge(setup_dve, nth(SETUP_DVE, "bounds"))
            for k in range(GROUPS):
                act.wait_ge(setup_pe, nth(SETUP_PE, f"woT{k}"))
                act.activation(WoT[:, k, :], bank(6 + k % 2), ACT.Copy, scale=kscale[:, 3:4]).then_inc(setup_act, 1)

            def ln(t):
                st = small[:, t.slot, :]
                act.wait_ge(p_shift, t.times(1, 1))
                wait(act, p_lo_ready, t.times(1, -3))
                wait(act, p_T_done, t.times(1, -3))
                act.activation(p_ln[:, t.slot, :], p_x[:, t.slot, :], ACT.Identity,
                               scale=st[:, 9:10], bias=st[:, 10:11]).then_inc(p_ln_ready, 1)

            def x_high(t):
                act.wait_ge(p_ln_ready, t.times(1, 1))
                act.activation(heads_of(t, qst, 0, HD), by_head(p_ln[:, t.slot, :]), ACT.Copy)\
                    .then_inc(p_hi_ready, 1)

            def xT(t):
                act.wait_ge(p_T_done, t.times(1, 1))
                wait(act, p_prod_ready, t.times(1, -1))
                wait(act, p_MN_done, t.times(1, -1))
                act.activation(p_xT[:, t.parity, :, :].rearrange("p g c -> p (g c)"), bank(0), ACT.Copy)\
                    .then_inc(p_xT_ready, 1)

            def root(t):
                st = small[:, t.slot, 16:]
                act.wait_ge(p_var_eps, t.times(1, 1))
                act.activation(st[:, 16:32], st[:, 0:16], ACT.Sqrt).then_inc(p_root_ready, 1)

            def key_high(t):
                act.wait_ge(p_key_ready, t.times(1, 1))
                act.activation(heads_of(t, kst, 0, HD), by_head(p_key[:, t.slot, :]), ACT.Copy)\
                    .then_inc(p_khi_ready, 1)

            def value_high(t):
                act.wait_ge(p_value_ready, t.times(1, 1))
                act.activation(heads_of(t, vst, 0, HD), by_head(p_value[:, t.slot, :]), ACT.Copy)\
                    .then_inc(p_vhi_ready, 1)

            pipelined(act, TILES, 4, [(1, ln), (3, root), (1, x_high), (1, xT), (4, key_high),
                                      (4, value_high)], peel=8)
            act.wait_ge(p_khi_ready, TILES)
            act.wait_ge(p_vhi_ready, TILES)
            act.wait_ge(p_xT_ready, TILES)
            act.wait_ge(setup_pe, nth(SETUP_PE, "bo"))
            act.activation(bo_all[:, :], bank(2), ACT.Copy).then_inc(setup_act, 1)
            act.wait_ge(setup_act, nth(SETUP_ACT, "bo"))
            act.activation(scratch[:, 20:21], ident[:, 0:1], ACT.Exp)
            act.sem_inc(projected, 1)

            def exps(h):
                act.wait_ge(shifted_done, h.times(1, 1))
                wait(act, prob_lo_ready, h.times(1, -1))
                act.activation(prob[:, h.parity, 0:1024], PS[:, 4:6, :].rearrange("p a t -> p (a t)"), ACT.Exp,
                               scale=kscale[:, 2:3])
                act.activation(prob[:, h.parity, 1024:1280], PS[:, 6, 0:256], ACT.Exp,
                               scale=kscale[:, 2:3]).then_inc(prob_ready, 1)
                act.wait_ge(prob_ready, h.times(1, 1))
                wait(act, pv_done, h.times(1, -1))
                act.activation(prob_parts[:, h.parity, 0, :], prob[:, h.parity, :], ACT.Copy)\
                    .then_inc(prob_hi_ready, 1)

            act.wait_ge(projected, 4)
            pipelined(act, UNITS, 8, [(0, exps)], peel=8)
            act.wait_ge(prob_hi_ready, UNITS)
            act.sem_inc(attended, 1)

            def stage_o(t):
                wait(act, o_T_done, t.times(1, -1))
                act.activation(by_head(o_in[:, t.parity, :]), heads_of(t, ost, 0, HD), ACT.Copy)\
                    .then_inc(o_staged, 1)

            def oT(t):
                act.wait_ge(o_T_done, t.times(1, 1))
                wait(act, o_proj_done, t.times(1, -1))
                act.activation(o_T[:, t.parity, :, :].rearrange("p g c -> p (g c)"), bank(0), ACT.Copy)\
                    .then_inc(o_T_ready, 1)

            def y_norm(t):
                st = small[:, t.slot, :]
                act.wait_ge(o_y_shift, t.times(1, 1))
                act.activation(o_y[:, t.slot, :], o_y[:, t.slot, :], ACT.Identity,
                               scale=st[:, 9:10], bias=st[:, 10:11]).then_inc(o_y_ln, 1)

            def x2_high(t):
                act.wait_ge(o_x2_ready, t.times(1, 1))
                wait(act, o_x2T_done, t.times(1, -1))
                act.activation(o_parts[:, t.parity, 0, :], o_x2[:, t.slot, :], ACT.Copy).then_inc(o_hi_ready, 1)

            def x2_T(t):
                act.wait_ge(o_x2T_done, t.times(1, 1))
                act.activation(x2T[:, :, bass.ds(t.times(P), P)],
                               bank16(7).rearrange("p (k c) -> p k c", c=P), ACT.Copy).then_inc(o_x2T_ready, 1)

            act.wait_ge(attended, 4)
            pipelined(act, TILES, 4, [(0, stage_o), (1, oT), (4, x2_high), (5, x2_T), (2, y_norm)], peel=8)
            act.wait_ge(o_x2T_ready, TILES)
            act.sem_inc(mixed, 1)

            act.wait_ge(mixed, 4)
            for primed in (silu_ready, fhi_ready, y_ln):
                act.sem_inc(primed, PRIMED)
            with act.Fori(0, BATCH) as c:
                act.wait_ge(down_done, c * CTILES + 1)
                with act.Fori(0, ITILES // 2) as j:
                    for u in range(2):
                        i = j * 2 + u
                        act.wait_ge(gate_done, c * ITILES + i + 1)
                        act.wait_ge(fuse_ready, c * ITILES + i + 1)
                        act.activation(f_silu[:, u, :], bank(u), ACT.Silu, scale=sgate[:, bass.ds(i, 1)])\
                            .then_inc(silu_ready, 1)
                        act.wait_ge(fuse_ready, c * ITILES + i + (1 + PRIMED))
                        act.activation(fused[:, 0, bass.ds(i, 1), :].rearrange("p a t -> p (a t)"),
                                       f_prod[:, u, :], ACT.Copy).then_inc(fhi_ready, 1)
                for u in range(CTILES):
                    st = small[:, u % 2, :]
                    act.wait_ge(y_rstd, c * CTILES + (u + 1))
                    act.activation(f_y[:, u % 2, :], f_y[:, u % 2, :], ACT.Identity,
                                   scale=st[:, 9:10], bias=st[:, 10:11]).then_inc(y_ln, 1)

        @block.vector
        def _(dve):
            links = [0]

            def link(ins):
                links[0] += 1
                ins.then_inc(setup_chain, 1)
                dve.wait_ge(setup_chain, links[0])

            def absolute(out, a):
                return dve.scalar_tensor_tensor(out, a, -1.0, a, ALU.mult, ALU.max)

            def x_stats(t):
                st = small[:, t.slot, :]
                arrived(dve, p_x_in, t)
                wait(dve, p_ln_ready, t.times(1, -3))
                dve.bn_stats(st[:, 0:6], p_x[:, t.slot, :]).then_inc(p_stats_chain, 1)

            def x_aggregate(t):
                st = small[:, t.slot, :]
                wait_apart(dve, p_stats_chain, t.times(2, 1), tally)
                dve.bn_aggr(st[:, 6:8], st[:, 0:6]).then_inc(p_stats_chain, 1)

            def x_var_eps(t):
                st = small[:, t.slot, :]
                dve.wait_ge(p_stats_chain, t.times(2, 2))
                dve.tensor_scalar(st[:, 8:9], st[:, 7:8], EPS, None, ALU.add).then_inc(p_stats, 1)

            def x_shift(t):
                st = small[:, t.slot, :]
                dve.wait_ge(p_rstd, t.times(1, 1))
                dve.scalar_tensor_tensor(st[:, 10:11], st[:, 6:7], -1.0, st[:, 9:10], ALU.mult, ALU.mult)\
                    .then_inc(p_shift, 1)

            def later(stage):
                return lambda t: None if t.loop is None and t.const < EARLY else stage(t)

            dve.memset(ones[:, :], 1.0).then_inc(setup_dve, 1)
            dve.memset(bdq, 0.0)
            dve.memset(bdo, 0.0).then_inc(setup_dve, 1)
            dve.memset(GMN[:, :, :, :], 0.0).then_inc(setup_dve, 1)
            dve.memset(negmax[:, :, :, :], 0.0)
            link(dve.memset(headsum[:, :], 0.0))
            for a in range(GH):
                dve.memset(headsum[HD * a:HD * a + HD, a:a + 1], 1.0)

            dve.wait_ge(wdkv_in, 16)
            dve.wait_ge(setup_pe, nth(SETUP_PE, "mean"))
            dve.scalar_tensor_tensor(wc, bank(0), -1.0 / LAT, wdkv_sb, ALU.mult, ALU.add).then_inc(setup_dve, 1)
            for name, n, dst in (("wukT", 1, wukT.rearrange("p g c -> p (g c)")), ("vecT", 5, vec[:, :]),
                                 ("bdqT", 3, bdqT.rearrange("p g c -> p (g c)"))):
                dve.wait_ge(setup_pe, nth(SETUP_PE, name))
                dve.tensor_copy(dst, PS[:, n, 0:dst.shape[1]]).then_inc(setup_dve, 1)
            dve.wait_ge(setup_dve, nth(SETUP_DVE, "vecT"))
            g, b = vec[:, 0:HEADS], vec[:, HEADS:2 * HEADS]
            absolute(scratch[:, 0:16], g)
            link(absolute(scratch[:, 16:32], b))
            link(dve.scalar_tensor_tensor(scratch[:, 32:48], scratch[:, 0:16], LATENT_MAX, scratch[:, 16:32],
                                          ALU.mult, ALU.add))
            for name, n, m in (("A", 6, absA), ("U", 7, absU)):
                dve.wait_ge(setup_pe, nth(SETUP_PE, name))
                link(dve.tensor_tensor(by_head(m), by_head(bank(n)), across(scratch[:, 32:48]), ALU.mult))
                absolute(m, m).then_inc(setup_dve, 1)
            dve.tensor_tensor(by_head(gA), by_head(bank(6)), across(g), ALU.mult).then_inc(setup_dve, 1)
            dve.tensor_tensor(by_head(gU), by_head(bank(7)), across(g), ALU.mult).then_inc(setup_dve, 1)

            for n, name, at, most in ((3, "keybound", 0, KEY_BOUND), (5, "valuebound", 3, VALUE_BOUND)):
                dve.wait_ge(setup_pe, nth(SETUP_PE, name))
                link(dve.tensor_reduce(kscale[:, at:at + 1], bank(n), AX.X, ALU.max))
                link(dve.tensor_scalar(kscale[:, at:at + 1], kscale[:, at:at + 1], 1e-30, 1.0 / most,
                                       ALU.max, ALU.mult))
            link(dve.reciprocal(kscale[:, 1:2], kscale[:, 0:1]))
            link(dve.tensor_scalar(kscale[:, 2:3], kscale[:, 0:1], 1.0 / math.sqrt(LAT), None, ALU.mult))
            dve.reciprocal(kscale[:, 4:5], kscale[:, 3:4]).then_inc(setup_dve, 1)
            dve.wait_ge(setup_dve, nth(SETUP_DVE, "bounds"))
            for m, name in ((1, "M"), (2, "N")):
                dve.wait_ge(setup_pe, nth(SETUP_PE, name))
                for a in range(GH):
                    rows = slice(HD * a, HD * a + HD)
                    last = dve.tensor_scalar(GMN[rows, :, m, rows], diagonal(m, rows),
                                             (kscale[rows, 1:2], kscale[rows, 4:5])[m - 1], None, ALU.mult)
                last.then_inc(setup_dve, 1)
            dve.tensor_tensor(by_head(bA), by_head(bank(6)), across(b), ALU.mult).then_inc(setup_dve, 1)
            dve.tensor_tensor(by_head(bU), by_head(bank(7)), across(b), ALU.mult).then_inc(setup_dve, 1)
            for t in range(EARLY):
                for stage in (x_stats, x_aggregate, x_var_eps):
                    stage(Step(4, None, t))
            for t in range(EARLY):
                x_shift(Step(4, None, t))
            dve.wait_ge(setup_pe, nth(SETUP_PE, "keybias"))
            dve.tensor_scalar(keybias[:, :], bank(4), kscale[:, 1:2], None, ALU.mult).then_inc(setup_dve, 1)
            dve.wait_ge(setup_pe, nth(SETUP_PE, "vb"))
            dve.tensor_scalar(vb_sb.rearrange("p g c -> p (g c)"), bank(5), kscale[:, 4:5], None, ALU.mult)\
                .then_inc(setup_dve, 1)

            link(dve.tensor_tensor(scratch[:, 0:16], vec[:, 32:48], vec[:, 48:64], ALU.mult))
            link(absolute(scratch[:, 0:16], scratch[:, 0:16]))
            dve.tensor_reduce(scratch[:, 16:17], scratch[:, 0:16], AX.X, ALU.max).then_inc(setup_dve, 1)
            dve.memset(vst[:, :, :, HD:VH], 1.0)
            dve.memset(vst[:, :, :, VW - 1:VW], 0.0).then_inc(setup_dve, 1)

            def product(t):
                dve.wait_ge(p_G_done, t.times(1, 1))
                wait(dve, p_var_done, t.times(1, -1))
                dve.tensor_tensor(p_prod[:, t.parity, :, :].rearrange("p g c -> p (g c)"), bank(1),
                                  p_xT[:, t.parity, :, :].rearrange("p g c -> p (g c)"), ALU.mult)\
                    .then_inc(p_prod_ready, 1)

            def newton(t):
                st = small[:, t.slot, 16:]
                return st[:, 0:16], st[:, 32:48], st[:, 48:64]

            def inverse(t):
                a, y, s = newton(t)
                dve.wait_ge(p_root_ready, t.times(1, 1))
                dve.reciprocal(y, small[:, t.slot, 32:48]).then_inc(p_newton_chain, 1)

            def squared(t):
                a, y, s = newton(t)
                dve.wait_ge(p_newton_chain, t.times(5, 1))
                dve.tensor_tensor(s, y, y, ALU.mult).then_inc(p_newton_chain, 1)

            def by_variance(t):
                a, y, s = newton(t)
                dve.wait_ge(p_newton_chain, t.times(5, 2))
                dve.tensor_tensor(s, s, a, ALU.mult).then_inc(p_newton_chain, 1)

            def correction(t):
                a, y, s = newton(t)
                dve.wait_ge(p_newton_chain, t.times(5, 3))
                dve.tensor_scalar(s, s, -0.5, 1.5, ALU.mult, ALU.add).then_inc(p_newton_chain, 1)

            def refined(t):
                a, y, s = newton(t)
                dve.wait_ge(p_newton_chain, t.times(5, 4))
                dve.tensor_tensor(y, y, s, ALU.mult).then_inc(p_newton_chain, 1)

            def key_raw(t):
                dve.wait_ge(p_newton_chain, t.times(5, 5))
                dve.wait_ge(p_MN_done, t.times(1, 1))
                wait(dve, p_klo_ready, t.times(1, -3))
                dve.tensor_tensor(by_head(p_key[:, t.slot, :]), by_head(bank(4 + t.parity)),
                                  across(small[:, t.slot, 48:64]), ALU.mult).then_inc(p_key_raw, 1)

            def var_eps(t):
                dve.wait_ge(p_var_done, t.times(1, 1))
                dve.tensor_scalar(small[:, t.slot, 16:32], bank(3)[:, 0:HEADS], 0.0, EPS, ALU.max, ALU.add)\
                    .then_inc(p_var_eps, 1)

            def value(t):
                wait(dve, p_vlo_ready, t.times(1, -3))
                dve.tensor_tensor(by_head(p_value[:, t.slot, :]), by_head(bank(6 + t.parity)),
                                  across(small[:, t.slot, 48:64]), ALU.mult).then_inc(p_value_ready, 1)

            def x_high_again(t):
                dve.wait_ge(p_hi_ready, t.times(1, 1))
                dve.tensor_copy(heads_of(t, qst, 2 * HD, STACK), heads_of(t, qst, 0, HD))

            def key_stack_rows(t):
                if t.loop is not None or t.const < TILES - 1:
                    return
                words = gmn_flat[STACK:P, 0:2 * SEQ].rearrange("p (b w) -> p b w", b=2)
                dve.wait_ge(p_MN_done, TILES)
                dve.memset(words[:, :, SEQ // 2:], 0.0).then_inc(key_rows, 1)
                dve.wait_ge(key_rows, 1)
                dve.memset(qk[STACK:STACK + 2, :, 1, :], 1.0).then_inc(key_rows, 1)

            def key_high_again(t):
                dve.wait_ge(p_khi_ready, t.times(1, 1))
                dve.tensor_copy(heads_of(t, kst, HD, 2 * HD), heads_of(t, kst, 0, HD))

            def key_low(t):
                dve.wait_ge(p_khi_ready, t.times(1, 1))
                dve.tensor_tensor(heads_of(t, kst, 2 * HD, STACK), by_head(p_key[:, t.slot, :]),
                                  heads_of(t, kst, 0, HD), ALU.subtract).then_inc(p_klo_ready, 1)

            pipelined(dve, TILES, 4, [(1, later(x_shift)), (0, later(x_stats)), (2, product), (3, inverse),
                                      (0, later(x_aggregate)), (2, x_high_again), (3, squared),
                                      (0, later(x_var_eps)), (4, key_stack_rows), (5, key_high_again),
                                      (3, by_variance), (5, key_low), (3, correction), (2, var_eps),
                                      (3, refined), (3, key_raw), (3, value)], peel=8)
            dve.wait_ge(p_klo_ready, TILES)
            dve.wait_ge(setup_pe, nth(SETUP_PE, "fuseT"))
            dve.tensor_reduce(scratch[0:1, 17:18], bank(0)[0:1, 0:P], AX.X, ALU.max).then_inc(setup_dve, 1)
            dve.sem_inc(projected, 1)

            dve.wait_ge(projected, 4)
            dve.wait_ge(setup_pe, nth(SETUP_PE, "fuseall"))
            dve.tensor_scalar(scratch[:, 18:19], bank(3)[:, 0:1], 1e-30, RAW_BOUND ** 2 / FUSE_BOUND,
                              ALU.max, ALU.mult).then_inc(setup_dve, 1)

            def maxima(h):
                if h.loop is None and h.const == 0:
                    dve.wait_ge(att_mask, 1)
                for s in SCORE_ORDER:
                    n, at = SCORE_AT[s]
                    if s == SCORE_ORDER[0]:
                        wait_apart(dve, scores_done, h.times(2, 1), tally)
                    elif s == SCORE_ORDER[1]:
                        wait_apart(dve, scores_done, h.times(2, 2), tally)
                    width = (s + 1) * P
                    last = dve.tensor_tensor_reduce(
                        out=PS[:, n, at:at + width], in0=PS[:, n, at:at + width], in1=causal[:, SEQ - width:],
                        scale=1.0, scalar=NEG, op0=ALU.add, op1=ALU.max,
                        accum_out=rowmax[:, h.parity, s:s + 1])
                last.then_inc(max_done, 1)

            def negmax_high(h):
                dve.wait_ge(max_done, h.times(1, 1))
                wait(dve, negmax_T, h.times(1, -1))
                dve.tensor_scalar(negmax[:, h.parity, :, 0], rowmax[:, h.parity, :], -1.0, None, ALU.mult)\
                    .then_inc(negmax_chain, 1)

            def negmax_low(h):
                dve.wait_ge(negmax_chain, h.times(1, 1))
                dve.scalar_tensor_tensor(negmax[:, h.parity, :, 1], rowmax[:, h.parity, :], -1.0,
                                         negmax[:, h.parity, :, 0], ALU.mult, ALU.subtract)\
                    .then_inc(negmax_ready, 1)

            def stacks(h):
                dve.wait_ge(stack_T, h.times(1, 1))
                wait(dve, shifted_done, h.times(1, -1))
                dve.tensor_copy(qk[0:STACK, h.parity, :, :].rearrange("p a t -> p (a t)"),
                                bank16(0)[0:STACK, :]).then_inc(stack_ready, 1)

            def negmax_rows(h):
                dve.wait_ge(negmax_T, h.times(1, 1))
                wait(dve, shifted_done, h.times(1, -1))
                dve.tensor_copy(qk[STACK:P, h.parity, 0, :], bank16(0)[STACK:P, 0:SEQ])\
                    .then_inc(negmax_stacked, 1)

            def sum_inverse(h):
                dve.wait_ge(pv_done, h.times(1, 1))
                wait(dve, o_stored, h.times(1, 0))
                dve.reciprocal(rsum[:, :], pv[:, :, HD]).then_inc(rsum_ready, 1)

            def normalise(h):
                dve.wait_ge(rsum_ready, h.times(1, 1))
                dve.tensor_tensor(ost[:, bass.ds(h.times(1), 1), :, :].rearrange("p a s c -> p (a s) c"),
                                  pv[:, :, 0:HD],
                                  rsum[:, :].unsqueeze(2).to_broadcast([P, SEQ_TILES, HD]), ALU.mult)\
                    .then_inc(o_stored, 1)

            pipelined(dve, UNITS, 8, [(1, maxima), (0, stacks), (1, negmax_high), (4, sum_inverse),
                                      (1, negmax_low), (4, normalise), (1, negmax_rows)], peel=8)
            dve.wait_ge(o_stored, UNITS)
            dve.sem_inc(attended, 1)

            def y(t):
                dve.wait_ge(o_proj_done, t.times(1, 1))
                wait(dve, o_x1_raw, t.times(1, -3))
                dve.tensor_tensor(o_y[:, t.slot, :], bank(1 + t.parity), bo_all[:, :], ALU.add)\
                    .then_inc(o_y_raw, 1)

            def y_bn(t):
                dve.wait_ge(o_y_raw, t.times(1, 1))
                dve.bn_stats(small[:, t.slot, 0:6], o_y[:, t.slot, :]).then_inc(o_y_chain, 1)

            def y_aggregate(t):
                wait_apart(dve, o_y_chain, t.times(2, 1), tally)
                dve.bn_aggr(small[:, t.slot, 6:8], small[:, t.slot, 0:6]).then_inc(o_y_chain, 1)

            def y_var_eps(t):
                dve.wait_ge(o_y_chain, t.times(2, 2))
                dve.tensor_scalar(small[:, t.slot, 8:9], small[:, t.slot, 7:8], EPS, None, ALU.add)\
                    .then_inc(o_y_stats, 1)

            def y_mean_shift(t):
                st = small[:, t.slot, :]
                dve.wait_ge(o_y_rstd, t.times(1, 1))
                dve.scalar_tensor_tensor(st[:, 10:11], st[:, 6:7], -1.0, st[:, 9:10], ALU.mult, ALU.mult)\
                    .then_inc(o_y_shift, 1)

            def x1(t):
                arrived(dve, o_x_in, t)
                dve.wait_ge(o_y_ln, t.times(1, 1))
                dve.tensor_tensor(heads_of(t, ost, 0, HD), by_head(o_y[:, t.slot, :]),
                                  by_head(o_x[:, t.slot, :]), ALU.add).then_inc(o_x1_raw, 1)

            def x1_bn(t):
                wait_apart(dve, o_x1_raw, t.times(1, 1), tally)
                dve.bn_stats(small[:, t.slot, 32:38], heads_of(t, ost, 0, HD)).then_inc(o_x1_chain, 1)

            def x1_aggregate(t):
                wait_apart(dve, o_x1_chain, t.times(2, 1), tally)
                dve.bn_aggr(small[:, t.slot, 38:40], small[:, t.slot, 32:38]).then_inc(o_x1_chain, 1)

            def x1_var_eps(t):
                dve.wait_ge(o_x1_chain, t.times(2, 2))
                dve.tensor_scalar(small[:, t.slot, 40:41], small[:, t.slot, 39:40], EPS, X2_SCALE ** -2,
                                  ALU.add, ALU.mult).then_inc(o_x1_stats, 1)

            def x1_mean_shift(t):
                st = small[:, t.slot, 32:]
                dve.wait_ge(o_x1_rstd, t.times(1, 1))
                dve.scalar_tensor_tensor(st[:, 10:11], st[:, 6:7], -1.0, st[:, 9:10], ALU.mult, ALU.mult)\
                    .then_inc(o_x1_shift, 1)

            def x2(t):
                st = small[:, t.slot, 32:]
                dve.wait_ge(o_x1_shift, t.times(1, 1))
                wait(dve, o_lo_ready, t.times(1, -3))
                dve.tensor_scalar(by_head(o_x2[:, t.slot, :]), heads_of(t, ost, 0, HD), st[:, 9:10],
                                  st[:, 10:11], ALU.mult, ALU.add).then_inc(o_x2_ready, 1)

            dve.wait_ge(setup_dve, nth(SETUP_DVE, "fusebound"))
            link(dve.reciprocal(scratch[:, 19:20], scratch[:, 18:19]))
            dve.tensor_scalar(sgate[:, :], vec[:, 32:48], 1.0 / X2_SCALE, None, ALU.mult)
            dve.tensor_scalar(sup[:, :], vec[:, 48:64], scratch[:, 19:20], 1.0 / X2_SCALE, ALU.mult, ALU.mult)
            dve.wait_ge(rows_in, 32)
            dve.tensor_scalar(sdown[:, :], sdown[:, :], scratch[:, 18:19], None, ALU.mult)
            dve.wait_ge(attended, 4)
            pipelined(dve, TILES, 4, [(2, y), (4, x1_mean_shift), (2, y_bn), (4, x2), (2, y_aggregate), (3, x1),
                                      (2, y_var_eps), (3, x1_bn), (2, y_mean_shift), (3, x1_aggregate),
                                      (3, x1_var_eps)], peel=8)
            dve.wait_ge(o_x2_ready, TILES)
            dve.sem_inc(mixed, 1)

            dve.wait_ge(mixed, 4)
            dve.sem_inc(fuse_ready, PRIMED)
            dve.sem_inc(y_read, PRIMED)
            dve.sem_inc(out_ready, 1)
            with dve.Fori(0, BATCH) as c:
                with dve.Fori(0, ITILES // 2) as j:
                    for u in range(2):
                        i = j * 2 + u
                        n = c * ITILES + i
                        dve.wait_ge(up_done, n + 1)
                        dve.wait_ge(silu_ready, n + (1 + PRIMED))
                        dve.wait_ge(flo_ready, n + 1)
                        dve.scalar_tensor_tensor(f_prod[:, u, :], bank(2 + u), sup[:, bass.ds(i, 1)],
                                                 f_silu[:, u, :], ALU.mult, ALU.mult).then_inc(fuse_ready, 1)

                def add_residual(u):
                    t = c * CTILES + u
                    dve.wait_ge(y_ln, t + (1 + PRIMED))
                    dve.tensor_tensor(by_head(f_out[:, u, :]), by_head(f_y[:, u % 2, :]),
                                      ost[:, bass.ds(c * HEADS, HEADS), u, :], ALU.add).then_inc(out_ready, 1)

                dve.wait_ge(chunk_stored, c + 1)
                for u in range(CTILES):
                    t = c * CTILES + u
                    st = small[:, u % 2, :]
                    dve.wait_ge(out_ready, c * CTILES + (max(u - 1, 0) + 1))
                    dve.wait_ge(down_done, t + 2)
                    dve.tensor_tensor(f_y[:, u % 2, :], bank(4 + u % 2), sdown[:, :], ALU.mult)\
                        .then_inc(y_read, 1)
                    dve.wait_ge(y_read, t + (1 + PRIMED))
                    dve.bn_stats(st[:, 0:6], f_y[:, u % 2, :]).then_inc(y_chain, 1)
                    wait_apart(dve, y_chain, t + 1, tally)
                    dve.bn_aggr(st[:, 6:8], st[:, 0:6]).then_inc(y_stats, 1)
                    if u:
                        add_residual(u - 1)
                add_residual(CTILES - 1)

        @block.tensor
        def _(pe):
            def transposes(n, src):
                for g in range(GROUPS):
                    last = pe.transpose(PS[:, n, P * g:P * g + P], src(g), ident[:, :])
                last.then_inc(setup_pe, 1)

            def products(n, lhs, rhs):
                for g in range(GROUPS):
                    last = pe.matmul(PS[:, n, P * g:P * g + P], lhs(g), rhs(g), start=True, stop=True)
                last.then_inc(setup_pe, 1)

            def tile_of(m):
                return lambda g: m[:, P * g:P * g + P]

            def group_of(m):
                return lambda g: m[:, g, :]

            pe.wait_ge(setup_dve, nth(SETUP_DVE, "ones"))
            pe.wait_ge(wdkv_in, 16)
            pe.matmul(bank(0), ones[:, :], wdkv_sb, start=True, stop=True).then_inc(setup_pe, 1)
            pe.wait_ge(consts_ready, 9)
            pe.wait_ge(heads_in, 32)
            transposes(1, tile_of(wuk_sb))
            transposes(2, tile_of(wuv_sb))
            pe.wait_ge(vecs_in, 64)
            pe.transpose(PS[:, 5, 0:64], vec_rows[0:64, :], ident[0:64, 0:64]).then_inc(setup_pe, 1)
            pe.wait_ge(blockdiag_in, 128)
            transposes(3, group_of(bdq))
            transposes(4, group_of(bdo))
            pe.wait_ge(setup_dve, nth(SETUP_DVE, "bdqT"))
            products(6, group_of(wukT), group_of(bdqT))
            pe.wait_ge(setup_act, nth(SETUP_ACT, "bdoT"))
            products(7, group_of(wuvT), group_of(bdoT))
            products(0, tile_of(wc), tile_of(wc))
            pe.wait_ge(setup_dve, nth(SETUP_DVE, "absA"))
            pe.matmul(bank(3), ones[:, :], absA, start=True, stop=True).then_inc(setup_pe, 1)
            pe.wait_ge(setup_dve, nth(SETUP_DVE, "absU"))
            pe.matmul(bank(5), ones[:, :], absU, start=True, stop=True).then_inc(setup_pe, 1)
            pe.wait_ge(setup_dve, nth(SETUP_DVE, "gA"))
            products(1, tile_of(wc), tile_of(gA))
            pe.wait_ge(setup_dve, nth(SETUP_DVE, "gU"))
            products(2, tile_of(wc), tile_of(gU))
            pe.wait_ge(setup_dve, nth(SETUP_DVE, "bA"))
            pe.matmul(bank(4), ones[:, :], bA, start=True, stop=True).then_inc(setup_pe, 1)
            pe.wait_ge(setup_dve, nth(SETUP_DVE, "bU"))
            products(5, tile_of(bU), lambda g: ones[:, :])
            pe.wait_ge(wo_in, 16)
            for k in range(GROUPS):
                if k >= 2:
                    pe.wait_ge(setup_act, nth(SETUP_ACT, f"woT{k - 2}"))
                transposes(6 + k % 2, lambda g: wo_nat[:, g, P * k:P * k + P])
            def keys_values(t):
                wait(pe, p_value_ready, t.times(1, -1))
                for m, n in ((1, 4), (2, 6)):
                    for g in range(GROUPS):
                        last = pe.matmul(PS[:, n + t.parity, P * g:P * g + P], p_xT[:, t.parity, g, :],
                                         GMN[:, g, m, :], start=True, stop=True)
                last.then_inc(p_MN_done, 1)

            def variance(t):
                pe.wait_ge(p_prod_ready, t.times(1, 1))
                wait(pe, p_var_eps, t.times(1, 0))
                for g in range(GROUPS):
                    last = pe.matmul(bank(3)[:, GH * g:GH * g + GH], p_prod[:, t.parity, g, :], headsum[:, :],
                                     start=True, stop=True)
                last.then_inc(p_var_done, 1)

            def xln_T(t):
                pe.wait_ge(p_ln_ready, t.times(1, 1))
                wait(pe, p_xT_ready, t.times(1, 0))
                for g in range(GROUPS):
                    last = pe.transpose(PS[:, 0, P * g:P * g + P], p_ln[:, t.slot, P * g:P * g + P],
                                        ident[:, :])
                last.then_inc(p_T_done, 1)

            def gram(t):
                pe.wait_ge(p_xT_ready, t.times(1, 1))
                wait(pe, p_prod_ready, t.times(1, 0))
                for g in range(GROUPS):
                    last = pe.matmul(PS[:, 1, P * g:P * g + P], GMN[:, g, 0, :], p_xT[:, t.parity, g, :],
                                     start=True, stop=True)
                last.then_inc(p_G_done, 1)

            pe.wait_ge(setup_dve, nth(SETUP_DVE, "done"))
            pe.wait_ge(setup_act, nth(SETUP_ACT, "G"))
            pipelined(pe, TILES, 4, [(2, keys_values), (1, xln_T), (2, variance), (1, gram)], peel=8)
            pe.wait_ge(p_xT_ready, TILES)
            pe.transpose(bank(0)[0:1, 0:P], scratch[:, 16:17], ident[:, :]).then_inc(setup_pe, 1)
            pe.wait_ge(setup_act, nth(SETUP_ACT, "woT3"))
            pe.wait_ge(rows_in, 32)
            pe.matmul(bank(2), ones[0:1, :], bo_all[0:1, :], start=True, stop=False)
            for g in range(GROUPS):
                last = pe.matmul(bank(2), vb_sb[:, g, :], WoT[:, g, :], start=False, stop=(g == GROUPS - 1))
            last.then_inc(setup_pe, 1)
            pe.wait_ge(setup_dve, nth(SETUP_DVE, "fusered"))
            pe.matmul(bank(3)[:, 0:1], ones[0:1, :], scratch[0:1, 17:18], start=True, stop=True)\
                .then_inc(setup_pe, 1)
            pe.wait_ge(p_MN_done, TILES)
            pe.wait_ge(p_var_done, TILES)
            pe.sem_inc(projected, 1)

            def score_tiles(h, tiles):
                for s in tiles:
                    n, at = SCORE_AT[s]
                    last = pe.matmul(PS[:, n, at:at + (s + 1) * P], qk[0:STACK, h.parity, 0, P * s:P * s + P],
                                     qk[0:STACK, h.parity, 1, 0:(s + 1) * P], start=True, stop=True)
                last.then_inc(scores_done, 1)

            def scores_first(h):
                if h.loop is None and h.const == 0:
                    pe.wait_ge(setup_dve, nth(SETUP_DVE, "fusebound"))
                pe.wait_ge(stack_ready, h.times(1, 1))
                wait(pe, max_done, h.times(1, 0))
                score_tiles(h, SCORE_ORDER[:1])

            def scores_rest(h):
                score_tiles(h, SCORE_ORDER[1:])

            def shifted(h):
                if h.loop is None and h.const == 0:
                    pe.wait_ge(key_rows, 2)
                pe.wait_ge(negmax_stacked, h.times(1, 1))
                wait(pe, prob_ready, h.times(1, 0))
                for t, (n, at) in enumerate(SHIFTED_AT):
                    pe.matmul(PS[:, n, at:at + SEQ - P * t], qk[:, h.parity, 1, P * t:P * t + P],
                              qk[:, h.parity, 0, P * t:SEQ], start=True, stop=False)
                    last = pe.matmul(PS[:, n, at:at + P], identb[:, :], causalT[:, :], start=False, stop=True)
                last.then_inc(shifted_done, 1)

            def weighted(h):
                pe.wait_ge(prob_lo_ready, h.times(1, 1))
                wait(pe, o_stored, h.times(1, 0))
                for s in range(SEQ_TILES):
                    for t in range(s + 1):
                        at = PROB_AT[t] + P * (s - t)
                        v = vst[:, bass.ds(h.times(1), 1), t, :].rearrange("p a c -> p (a c)")
                        for n, (part, lo) in enumerate(((0, 0), (0, VH), (1, 0))):
                            last = pe.matmul(pv[:, s, :],
                                             prob_parts[:, h.parity, part, at:at + P], v[:, lo:lo + VH],
                                             start=(t == 0 and n == 0), stop=(t == s and n == 2))
                last.then_inc(pv_done, 1)

            def stack_transposes(h):
                wait(pe, stack_ready, h.times(1, 0))
                for a, stack in enumerate((qst, kst)):
                    for s in range(SEQ_TILES):
                        last = pe.transpose(bank16(0)[0:STACK, SEQ * a + P * s:SEQ * a + P * s + P],
                                            stack[:, bass.ds(h.times(1), 1), s, :].rearrange("p a c -> p (a c)"),
                                            ident16[:, :])
                last.then_inc(stack_T, 1)

            def negmax_transposes(h):
                pe.wait_ge(negmax_ready, h.times(1, 1))
                wait(pe, negmax_stacked, h.times(1, 0))
                for s in range(SEQ_TILES):
                    last = pe.transpose(bank16(0)[STACK:P, P * s:P * s + P], negmax[:, h.parity, s, :],
                                        ident16[:, :])
                last.then_inc(negmax_T, 1)

            pe.wait_ge(projected, 4)
            pipelined(pe, UNITS, 8, [(1, scores_first), (2, negmax_transposes), (1, scores_rest),
                                     (0, stack_transposes), (2, shifted), (4, weighted)], peel=8)
            pe.wait_ge(pv_done, UNITS)
            pe.sem_inc(attended, 1)

            def project(t):
                pe.wait_ge(o_T_ready, t.times(1, 1))
                wait(pe, o_y_raw, t.times(1, -1))
                for g in range(GROUPS):
                    last = pe.matmul(bank(1 + t.parity), o_T[:, t.parity, g, :], WoT[:, g, :],
                                     start=(g == 0), stop=(g == GROUPS - 1))
                last.then_inc(o_proj_done, 1)

            def o_transposes(t):
                pe.wait_ge(o_staged, t.times(1, 1))
                wait(pe, o_T_ready, t.times(1, 0))
                for g in range(GROUPS):
                    last = pe.transpose(PS[:, 0, P * g:P * g + P], o_in[:, t.parity, P * g:P * g + P],
                                        ident[:, :])
                last.then_inc(o_T_done, 1)

            def x2_transposes(t):
                pe.wait_ge(o_lo_ready, t.times(1, 1))
                wait(pe, o_x2T_ready, t.times(1, 0))
                for part in range(2):
                    for k in range(GROUPS):
                        at = P * (part * GROUPS + k)
                        last = pe.transpose(bank16(7)[:, at:at + P], o_parts[:, t.parity, part, P * k:P * k + P],
                                            ident16[:, :])
                last.then_inc(o_x2T_done, 1)

            def hidden(m, i, u, c):
                for k in range(GROUPS):
                    for part in range(2):
                        last = pe.matmul(bank(2 * m + u), w_gu[:, m, k, bass.ds(i * P, P)],
                                         x2T[:, part * GROUPS + k, bass.ds(c * CHUNK, CHUNK)],
                                         start=(k == 0 and part == 0), stop=(k == GROUPS - 1 and part == 1))
                last.then_inc((gate_done, up_done)[m], 1)

            def hidden_early(t):
                if t.loop is not None or t.const < TILES - 3:
                    return
                n = t.const - (TILES - 3)
                if n == 0:
                    pe.wait_ge(wffn_in, 48)
                    pe.wait_ge(o_x2T_ready, CTILES)
                    pe.wait_ge(o_T_ready, TILES)
                    pe.wait_ge(o_y_raw, TILES)
                hidden(n % 2, n // 2, n // 2, 0)

            pe.wait_ge(attended, 4)
            pipelined(pe, TILES, 4, [(1, o_transposes), (2, project), (5, hidden_early), (5, x2_transposes)],
                      peel=8)
            pe.wait_ge(o_x2T_done, TILES)
            pe.sem_inc(mixed, 1)
            hidden(1, 1, 1, 0)

            def hidden_pair(c, j):
                for u in range(2):
                    i = j * 2 + u
                    for m, free in enumerate((silu_ready, fuse_ready)):
                        pe.wait_ge(free, c * ITILES + i + 1)
                        hidden(m, i, u, c)

            def down(c):
                for u in range(CTILES):
                    pe.wait_ge(y_read, c * CTILES + (u + 1))
                    for i in range(ITILES):
                        if u == 0 and i in (0, ITILES - 2, ITILES - 1):
                            pe.wait_ge(flo_ready, c * ITILES + (max(i + 1, ITILES - 2) + PRIMED))
                        for part in range(2):
                            last = pe.matmul(bank(4 + u % 2), fused[:, part, i, P * u:P * u + P], w_dn[:, i, :],
                                             start=(i == 0 and part == 0), stop=(i == ITILES - 1 and part == 1))
                    last.then_inc(down_done, 1)

            pe.wait_ge(mixed, 4)
            pe.sem_inc(down_done, 1)
            with pe.Fori(1, ITILES // 2) as j:
                hidden_pair(0, j)
            down(0)
            with pe.Fori(1, BATCH) as c:
                with pe.Fori(0, ITILES // 2) as j:
                    hidden_pair(c, j)
                down(c)


_INS = ["L0_attn_x", "L0_attn_Wq", "L0_attn_Wdkv", "L0_attn_Wuk", "L0_attn_Wuv", "L0_attn_ln_g", "L0_attn_ln_b",
        "L0_attn_Wo_h", "L0_attn_Wo", "L0_attn_bo", "L0_ffn_w_gate", "L0_ffn_w_up", "L0_ffn_w_down",
        "L0_ffn_s_gate", "L0_ffn_s_up", "L0_ffn_s_down"]


def kernel(**inputs):
    import numpy as np
    import concourse.bacc as bacc
    from concourse.bass_utils import run_bass_kernel_spmd

    nc = bacc.Bacc("TRN2", target_bir_lowering=False, num_devices=1)
    arrays, args = {}, []
    for name in _INS:
        a = np.ascontiguousarray(inputs[name])
        if a.dtype.itemsize == 1:
            a = a.view(np.int32)
        arrays[f"in_{name}"] = a
        args.append(nc.dram_tensor(f"in_{name}", a.shape, mybir.dt.from_np(a.dtype), kind="ExternalInput").ap())
    args.append(nc.dram_tensor("out_x", (BATCH, SEQ, EMB), mybir.dt.float32, kind="ExternalOutput").ap())
    block_kernel(nc, *args)
    r = run_bass_kernel_spmd(nc, [arrays], core_ids=[0])
    return r.results[0]["out_x"]
```
